# Optimizing a Trainium2 kernel written in Bass

```python
import numpy as np
import jax
import jax.numpy as jnp

def _softmax(x, axis=-1):
    return jax.nn.softmax(x, axis=axis)

def _gelu(x):
    return jax.nn.gelu(x, approximate=True)

def _silu(x):
    return jax.nn.silu(x)

def _sigmoid(x):
    return jax.nn.sigmoid(x)

def _layernorm(x, axis=-1, eps=1e-05):
    m = jnp.mean(x, axis=axis, keepdims=True)
    v = jnp.var(x, axis=axis, keepdims=True)
    return (x - m) / jnp.sqrt(v + eps)

def _scatter_add(tgt, idx, src, axis=0):
    return tgt.at[idx].add(src)

def _segment_sum(src, seg, n):
    return jax.ops.segment_sum(src, seg, n)
kernel_name = 'mk_vit_tower_d1_tok_img512_r4_a38f97'

def setup_inputs(seed: int=0):
    np.random.seed(seed)
    _w = jnp.asarray

    def _rec_inputs():
        import jax
        import jax.numpy as jnp
        _rk = jax.random.key(seed)
        x = 7.57192e-06 + 1.00007 * jax.random.normal(jax.random.fold_in(_rk, 1), (128, 64, 64, 3), jnp.float32)
        return x
    x = _rec_inputs()

    def _L0_tok_setup():
        import jax, jax.numpy as jnp
        import numpy as np
        B, H, W, C = (64, 224, 224, 3)
        P, D = (16, 128)
        LN_EPS = 0.001

        def _shift4(x):
            pad = lambda a, spec: jnp.pad(a, spec)
            right = pad(x[:, :, :-1, :], ((0, 0), (0, 0), (1, 0), (0, 0)))
            left = pad(x[:, :, 1:, :], ((0, 0), (0, 0), (0, 1), (0, 0)))
            down = pad(x[:, :-1, :, :], ((0, 0), (1, 0), (0, 0), (0, 0)))
            up = pad(x[:, 1:, :, :], ((0, 0), (0, 1), (0, 0), (0, 0)))
            return [right, left, down, up]
        key = jax.random.key(seed)
        k0, k1, k2 = jax.random.split(key, 3)
        x = jax.random.normal(k0, (B, H, W, C), jnp.float32)
        conv_w = jax.random.normal(k1, (P, P, 5 * C, D), jnp.float32) * 0.02
        conv_b = jnp.zeros((D,), jnp.float32)
        gamma = jnp.ones((D,), jnp.float32)
        beta = jnp.zeros((D,), jnp.float32)
        dense_w = jax.random.normal(k2, (D, D), jnp.float32) * 0.02
        dense_b = jnp.zeros((D,), jnp.float32)
        return {'x': x, 'conv_w': conv_w, 'conv_b': conv_b, 'gamma': gamma, 'beta': beta, 'dense_w': dense_w, 'dense_b': dense_b}
    _L0_tok_all = _L0_tok_setup()
    _L0_tok_in = {k: v for k, v in _L0_tok_all.items() if k in ('conv_w', 'conv_b', 'gamma', 'beta', 'dense_w', 'dense_b')}
    del _L0_tok_all

    def _L0_attn_setup():
        import jax, jax.numpy as jnp
        import numpy as np
        import math
        HEADS = 8
        key = jax.random.key(seed)
        ks = jax.random.split(key, 9)
        B, T, E = (2, 512, 128)
        s = 1.0 / math.sqrt(E)
        return {'x': jax.random.normal(ks[0], (B, T, E), jnp.float32), 'wq': jax.random.normal(ks[1], (E, E), jnp.float32) * s, 'bq': jax.random.normal(ks[2], (E,), jnp.float32) * s, 'wk': jax.random.normal(ks[3], (E, E), jnp.float32) * s, 'bk': jax.random.normal(ks[4], (E,), jnp.float32) * s, 'wv': jax.random.normal(ks[5], (E, E), jnp.float32) * s, 'bv': jax.random.normal(ks[6], (E,), jnp.float32) * s, 'wg': jax.random.normal(ks[7], (E, E), jnp.float32) * s, 'bg': jax.random.normal(ks[8], (E,), jnp.float32) * s}
    _L0_attn_all = _L0_attn_setup()
    _L0_attn_in = {k: v for k, v in _L0_attn_all.items() if k in ('wq', 'bq', 'wk', 'bk', 'wv', 'bv', 'wg', 'bg')}
    del _L0_attn_all

    def _L0_ffn_setup():
        import jax, jax.numpy as jnp
        import numpy as np
        E = 64
        K = 2
        D = 128
        H = 64
        NSH = 2
        ROUTE_SCALE = 2.5
        CAP = 256
        STD = 0.02
        key = jax.random.key(seed)
        ks = jax.random.split(key, 8)
        x = jax.random.normal(ks[0], (4, 512, D), dtype=jnp.float32)
        gate_w = jax.random.normal(ks[1], (E, D), dtype=jnp.float32) * STD
        w1 = jax.random.normal(ks[2], (E, D, H), dtype=jnp.float32) * STD
        w3 = jax.random.normal(ks[3], (E, D, H), dtype=jnp.float32) * STD
        w2 = jax.random.normal(ks[4], (E, H, D), dtype=jnp.float32) * STD
        sw1 = jax.random.normal(ks[5], (D, H * NSH), dtype=jnp.float32) * STD
        sw3 = jax.random.normal(ks[6], (D, H * NSH), dtype=jnp.float32) * STD
        sw2 = jax.random.normal(ks[7], (H * NSH, D), dtype=jnp.float32) * STD
        return {'x': x, 'gate_w': gate_w, 'w1': w1, 'w3': w3, 'w2': w2, 'sw1': sw1, 'sw3': sw3, 'sw2': sw2}
    _L0_ffn_all = _L0_ffn_setup()
    _L0_ffn_in = {k: v for k, v in _L0_ffn_all.items() if k in ('gate_w', 'w1', 'w3', 'w2', 'sw1', 'sw3', 'sw2')}
    del _L0_ffn_all
    return {'x': x, 'L0_tok_conv_w': _L0_tok_in['conv_w'], 'L0_tok_conv_b': _L0_tok_in['conv_b'], 'L0_tok_gamma': _L0_tok_in['gamma'], 'L0_tok_beta': _L0_tok_in['beta'], 'L0_tok_dense_w': _L0_tok_in['dense_w'], 'L0_tok_dense_b': _L0_tok_in['dense_b'], 'L0_attn_wq': _L0_attn_in['wq'], 'L0_attn_bq': _L0_attn_in['bq'], 'L0_attn_wk': _L0_attn_in['wk'], 'L0_attn_bk': _L0_attn_in['bk'], 'L0_attn_wv': _L0_attn_in['wv'], 'L0_attn_bv': _L0_attn_in['bv'], 'L0_attn_wg': _L0_attn_in['wg'], 'L0_attn_bg': _L0_attn_in['bg'], 'L0_ffn_gate_w': _L0_ffn_in['gate_w'], 'L0_ffn_w1': _L0_ffn_in['w1'], 'L0_ffn_w3': _L0_ffn_in['w3'], 'L0_ffn_w2': _L0_ffn_in['w2'], 'L0_ffn_sw1': _L0_ffn_in['sw1'], 'L0_ffn_sw3': _L0_ffn_in['sw3'], 'L0_ffn_sw2': _L0_ffn_in['sw2']}

def reference(x, L0_tok_conv_w, L0_tok_conv_b, L0_tok_gamma, L0_tok_beta, L0_tok_dense_w, L0_tok_dense_b, L0_attn_wq, L0_attn_bq, L0_attn_wk, L0_attn_bk, L0_attn_wv, L0_attn_bv, L0_attn_wg, L0_attn_bg, L0_ffn_gate_w, L0_ffn_w1, L0_ffn_w3, L0_ffn_w2, L0_ffn_sw1, L0_ffn_sw3, L0_ffn_sw2):
    import jax
    import jax.numpy as jnp

    def _L0_tok_ref(x, conv_w, conv_b, gamma, beta, dense_w, dense_b):
        import jax, jax.numpy as jnp
        import numpy as np
        B, H, W, C = (64, 224, 224, 3)
        P, D = (16, 128)
        LN_EPS = 0.001

        def _shift4(x):
            pad = lambda a, spec: jnp.pad(a, spec)
            right = pad(x[:, :, :-1, :], ((0, 0), (0, 0), (1, 0), (0, 0)))
            left = pad(x[:, :, 1:, :], ((0, 0), (0, 0), (0, 1), (0, 0)))
            down = pad(x[:, :-1, :, :], ((0, 0), (1, 0), (0, 0), (0, 0)))
            up = pad(x[:, 1:, :, :], ((0, 0), (0, 1), (0, 0), (0, 0)))
            return [right, left, down, up]
        xs = jnp.concatenate([x, *_shift4(x)], axis=-1)
        y = jax.lax.conv_general_dilated(xs, conv_w, window_strides=(P, P), padding='VALID', dimension_numbers=('NHWC', 'HWIO', 'NHWC')) + conv_b
        y = y.reshape(y.shape[0], -1, D)
        mu = jnp.mean(y, axis=-1, keepdims=True)
        var = jnp.mean(jnp.square(y - mu), axis=-1, keepdims=True)
        y = (y - mu) * jax.lax.rsqrt(var + LN_EPS) * gamma + beta
        return y @ dense_w + dense_b

    def _L0_attn_ref(x, wq, bq, wk, bk, wv, bv, wg, bg):
        import jax, jax.numpy as jnp
        import numpy as np
        import math
        HEADS = 8
        B, T, E = x.shape
        H = HEADS
        D = E // H
        gammas = 1.0 - 2.0 ** (-5.0 - jnp.arange(H, dtype=jnp.float32))
        q = (x @ wq.T + bq).reshape(B, T, H, D)
        k = (x @ wk.T + bk).reshape(B, T, H, D)
        v = (x @ wv.T + bv).reshape(B, T, H, D)
        idx = jnp.arange(T)
        rel = idx[None, :] - idx[:, None]
        decay = jnp.where(rel[None] >= 0, gammas[:, None, None] ** rel[None].astype(jnp.float32), 0.0)
        scores = jnp.einsum('bihd,bjhd->bhij', q, k) / math.sqrt(D)
        scores = scores * decay[None]
        out = jnp.einsum('bhij,bjhd->bihd', scores, v).reshape(B, T, E)
        gate = jax.nn.silu(x @ wg.T + bg)
        return gate * out

    def _L0_ffn_ref(x, gate_w, w1, w3, w2, sw1, sw3, sw2):
        import jax, jax.numpy as jnp
        import numpy as np
        E = 64
        K = 2
        D = 128
        H = 64
        NSH = 2
        ROUTE_SCALE = 2.5
        CAP = 256
        STD = 0.02
        bs, slen, d = x.shape
        xf = x.reshape(-1, d)
        logits = xf @ gate_w.T
        scores = jax.nn.sigmoid(logits.astype(jnp.float32))
        top_scores, top_idx = jax.lax.top_k(scores, K)
        top_scores = top_scores / (top_scores.sum(-1, keepdims=True) + 1e-20)
        top_scores = top_scores * ROUTE_SCALE
        flat_e = top_idx.reshape(-1)
        x_pairs = jnp.repeat(xf, K, axis=0)
        oh = jax.nn.one_hot(flat_e, E, dtype=jnp.int32)
        pos = jnp.take_along_axis(jnp.cumsum(oh, axis=0), flat_e[:, None], axis=1)[:, 0] - 1
        buf = jnp.zeros((E, CAP, d), dtype=xf.dtype).at[flat_e, pos].set(x_pairs, mode='drop')
        h = jax.nn.silu(jnp.einsum('ecd,edh->ech', buf, w1)) * jnp.einsum('ecd,edh->ech', buf, w3)
        y = jnp.einsum('ech,ehd->ecd', h, w2)
        valid = (pos < CAP)[:, None]
        y_pairs = jnp.where(valid, y[flat_e, jnp.minimum(pos, CAP - 1)], 0.0)
        routed = (y_pairs.reshape(-1, K, d) * top_scores[..., None].astype(xf.dtype)).sum(axis=1)
        shared = jax.nn.silu(xf @ sw1) * (xf @ sw3) @ sw2
        return (shared + routed).reshape(bs, slen, d)
    h = _L0_tok_ref(x, L0_tok_conv_w, L0_tok_conv_b, L0_tok_gamma, L0_tok_beta, L0_tok_dense_w, L0_tok_dense_b)
    h = h + _L0_attn_ref(_layernorm(h, axis=-1), L0_attn_wq, L0_attn_bq, L0_attn_wk, L0_attn_bk, L0_attn_wv, L0_attn_bv, L0_attn_wg, L0_attn_bg)
    h = h + _L0_ffn_ref(_layernorm(h, axis=-1), L0_ffn_gate_w, L0_ffn_w1, L0_ffn_w3, L0_ffn_w2, L0_ffn_sw1, L0_ffn_sw3, L0_ffn_sw2)
    return h

_drawn_inputs = setup_inputs


def setup_inputs(seed=0):
    import zlib

    import numpy as np

    out = dict(_drawn_inputs(seed))
    spreads = {'L0_tok_conv_b': (0.0, 0.1),
     'L0_tok_gamma': (1.0, 0.2),
     'L0_tok_beta': (0.0, 0.1),
     'L0_tok_dense_b': (0.0, 0.1)}
    factors = {'L0_ffn_gate_w': 8.0,
     'L0_ffn_w1': 8.0,
     'L0_ffn_w3': 8.0,
     'L0_ffn_w2': 8.0,
     'L0_ffn_sw1': 8.0,
     'L0_ffn_sw3': 8.0,
     'L0_ffn_sw2': 8.0}
    for name, (base, spread) in spreads.items():
        noise = np.random.default_rng([zlib.crc32(name.encode()), seed]).standard_normal(out[name].shape)
        drawn = base * np.exp(spread * noise) if base else spread * noise
        out[name] = jnp.asarray(drawn.astype(out[name].dtype))
    for name, factor in factors.items():
        out[name] = (out[name] * factor).astype(out[name].dtype)
    return out
```

```python
from contextlib import ExitStack

import numpy as np

import concourse.bass as bass
from concourse import mybir

F32 = mybir.dt.float32
BF16 = mybir.dt.bfloat16
I32 = mybir.dt.int32
U32 = mybir.dt.uint32
ALU = mybir.AluOpType
ACT = mybir.ActivationFunctionType
AX = mybir.AxisListType

P = 128
IMAGES, SIDE, CH = 128, 64, 3
PATCH = 16
GRID = SIDE // PATCH
T = GRID * GRID
TOKENS = IMAGES * T
NT = TOKENS // P
TG = 4
NG = NT // TG
GN = TG * P
GB = IMAGES // NG
KP = PATCH * PATCH * CH
NCH = KP // P
EDGE = PATCH * CH
HEADS = 8
HD = P // HEADS
QM = 4
NE = 64
TOPK = 2
CAP = 256
HID = 64
BLK = 128
EG = 4
NEG = NE // EG
NOV = 32
ROW = P + 2
BIG = 1 << 20
LN_TOK, LN = 1e-3, 1e-5
ROUTE_SCALE = 2.5
assert (TOKENS * TOPK) // (BLK + 1) < NOV


def constants():
    ident = np.eye(P, dtype=np.float32)
    center = ident - np.float32(1.0 / P)
    gam = (1.0 - 2.0 ** (-5.0 - np.arange(HEADS, dtype=np.float32))).astype(np.float32)
    j, i = np.arange(P)[:, None], np.arange(P)[None, :]
    keep = (j // T == i // T) & (j >= i)
    decay = np.zeros((P, HEADS, P), np.float32)
    for h in range(HEADS):
        decay[:, h] = np.where(keep, gam[h] ** np.maximum(j - i, 0).astype(np.float32), 0.0)
    decay *= np.float32(HD ** -0.5)
    before = (j < i).astype(np.float32)
    expert = np.broadcast_to(np.arange(NE, dtype=np.float32), (P, NE))
    left = np.broadcast_to(NE - np.arange(NE, dtype=np.float32), (P, NE))
    head = (np.arange(P)[:, None] // HD % QM == np.arange(QM)[None, :]).astype(np.float32)
    flat = np.concatenate([ident, center, before, expert, left, head, decay.reshape(P, -1)], 1)
    token = np.arange(NT)[None, :, None] * P + np.arange(P)[:, None, None]
    dest = (token * TOPK + np.arange(TOPK)[None, None, :]).astype(np.int32).reshape(P, NT * TOPK)
    return np.ascontiguousarray(flat, np.float32), np.ascontiguousarray(dest)


NC_CONST = 3 * P + 2 * NE + QM + HEADS * P


def tower(nc, xp, xe, wp, we, sq, w13, w2, vecs, rows, cst, dest, out):
    ctx = ExitStack()
    with ctx:
        def sb(name, shape, dt=F32):
            return ctx.enter_context(nc.sbuf_tensor(name, shape, dt))

        def sem(name):
            return ctx.enter_context(nc.semaphore(name))

        buf = nc.dram_tensor("expert_rows", ((NE + 1) * CAP, ROW), F32, kind="Internal").ap()
        pair = nc.dram_tensor("pair_rows", (TOKENS * TOPK, P), F32, kind="Internal").ap()

        C = sb("C", [P, NC_CONST])
        ident = C[:, 0:P]
        center = C[:, P:2 * P]
        before_f = C[:, 2 * P:3 * P]
        expert = C[:, 3 * P:3 * P + NE]
        left = C[:, 3 * P + NE:3 * P + 2 * NE]
        head = C[:, 3 * P + 2 * NE:3 * P + 2 * NE + QM]
        decay = C[:, 3 * P + 2 * NE + QM:NC_CONST]
        destv = sb("destv", [P, NT, TOPK], I32)
        V = sb("V", [P, 5])
        conv_b, gamma, beta, bq, bk = (V[:, n:n + 1] for n in range(5))
        R = sb("R", [P, 3 * P])
        vg_bias, dense_bias = R[:, 0:2 * P], R[:, 2 * P:3 * P]
        SQ = sb("SQ", [P, 8 * P + NE])
        dw, wq, wk, wvg, s1, s3, s2, gw = (SQ[:, a:b] for a, b in (
            (0, P), (P, 2 * P), (2 * P, 3 * P), (3 * P, 5 * P), (5 * P, 6 * P), (6 * P, 7 * P),
            (7 * P, 8 * P), (8 * P, 8 * P + NE)))
        WP = sb("WP", [P, 2, 5, NCH // 2, P])
        W = sb("W", [P, NCH, P])
        WE = sb("WE", [2 * EDGE, 2, P])
        gdw = sb("gdw", [P, P])
        WD = sb("WD", [P, P])
        betab = sb("betab", [P, P])
        cvec = sb("cvec", [P, P])
        bqm = sb("bqm", [P, QM])
        before = sb("before", [P, P], BF16)
        ones = sb("ones", [P, P], BF16)
        mhalf = sb("mhalf", [P, 1])
        FILLR = 16
        fill = sb("fill", [P, FILLR, ROW])
        zero = sb("zero", [P, 2048])

        XR = 8
        X = sb("X", [P, 2, NCH, GN])
        XE = sb("XE", [2 * EDGE, 2, 2, GN])
        yT = sb("yT", [P, 2, GN])
        h = sb("h", [P, NT, P])
        x2T = sb("x2T", [P, NT, P])
        st1, st2, st3 = (sb(f"st{n}", [P, 2, 6]) for n in (1, 2, 3))
        mv1, mv2, mv3 = (sb(f"mv{n}", [P, 2, 2]) for n in (1, 2, 3))
        ve1, ve2, ve3 = (sb(f"ve{n}", [P, 2, 1]) for n in (1, 2, 3))
        rs1, rs2, rs3 = (sb(f"rs{n}", [P, 2, 1]) for n in (1, 2, 3))
        xn = sb("xn", [P, 2, P])
        xnT = sb("xnT", [P, 2, P])
        qm = sb("qm", [P, 2, QM, P])
        kT = sb("kT", [P, 2, P])
        vg = sb("vg", [P, 4, 2 * P])
        ST = sb("ST", [P, 2, HEADS, P])
        go = sb("go", [P, P])
        xrow = sb("xrow", [P, XR, TOPK, ROW])
        th = sb("th", [P, 2, NE])
        sg = sb("sg", [P, NE])
        top = sb("top", [P, 8])
        topi = sb("topi", [P, 8], U32)
        idx = sb("idx", [P, 4, TOPK])
        OH = sb("OH", [P, 4, TOPK, NE], BF16)
        acc = sb("acc", [P, 3, NE], BF16)
        ssum = sb("ssum", [P, 1])
        srec = sb("srec", [P, 1])
        mpos = sb("mpos", [P, TOPK, NE])
        pos = sb("pos", [P, TOPK])
        over = sb("over", [P, TOPK])
        place = sb("place", [P, TOPK])
        slots = sb("slots", [P, TOPK, NT], U32)

        NW = 6
        NY = 4
        xb = sb("xb", [P, NW, EG, ROW])
        w13s = sb("w13s", [P, NW, EG, P])
        w2s = sb("w2s", [P, NW, EG, P])
        xbT = sb("xbT", [P, 2, EG, BLK])
        gs = sb("gs", [P, 2, EG * BLK])
        hT = sb("hT", [P, 2, EG, BLK])
        ys = sb("ys", [P, NY, EG, P])
        shg = sb("shg", [P, GN])
        shT = sb("shT", [P, TG, P])
        ovv = sb("ovv", [P, NE])
        ovw = sb("ovw", [P, NE])
        ovl = sb("ovl", [P, NOV])
        ovf = sb("ovf", [P, NOV])
        ovrow = sb("ovrow", [P, NOV], I32)
        ovexp = sb("ovexp", [P, NOV], I32)
        ovc = sb("ovc", [P, 8])
        ovs = sb("ovs", [P, 1])
        ovn = sb("ovn", [P, 1], I32)
        pr = X[:, :, :, :].rearrange("p a c n -> p (a c n)")[:, 0:NT * TOPK * P].rearrange(
            "p (t k d) -> p t k d", t=NT, k=TOPK)

        bank = [ctx.enter_context(nc.psum_tensor(f"bank{n}", [P, 512], F32)) for n in range(8)]
        CONV, A, TR, QK, VG, S0, S1, O = bank
        XT = bank[0:2]
        GU = bank[2:4]
        Y = bank[4:6]
        SH1, SH3 = bank[6:8]

        c_in, v_in, r_in, sq_in, we_in = sem("c_in"), sem("v_in"), sem("r_in"), sem("sq_in"), sem("we_in")
        wp_in = [sem("wp_in0"), sem("wp_in1")]
        x_in = [[sem(f"x_in{n}_{part}") for part in range(3)] for n in range(2)]
        filled_tile, filled = sem("filled_tile"), sem("filled")
        ones_set = sem("ones_set")
        w_ready, wd_in_ready, wd_ps, wd_ready, cvec_ready, bqm_ready, before_ready = (sem(n) for n in (
            "w_ready", "wd_in_ready", "wd_ps", "wd_ready", "cvec_ready", "bqm_ready", "before_ready"))
        conv_ps, yT_ready = sem("conv_ps"), sem("yT_ready")
        y_ps, ystat, r1_ready, h_ready, hstat, r2_ready = (sem(n) for n in (
            "y_ps", "ystat", "r1_ready", "h_ready", "hstat", "r2_ready"))
        xn_ready, xnT_ps, xnT_ready = sem("xn_ready"), sem("xnT_ps"), sem("xnT_ready")
        qk_ps, vg_ps, qk_ready, vg_ready, g_ready = (sem(n) for n in (
            "qk_ps", "vg_ps", "qk_ready", "vg_ready", "g_ready"))
        s_ps, st_ready, av_ps, av_read, h2stat, r3_ready, h2_ready = (sem(n) for n in (
            "s_ps", "st_ready", "av_ps", "av_read", "h2stat", "r3_ready", "h2_ready"))
        xf_ready, x2T_ps, x2T_ready, lg_ps, th_ready, oh_ready, meta_ready = (sem(n) for n in (
            "xf_ready", "x2T_ps", "x2T_ready", "lg_ps", "th_ready", "oh_ready", "meta_ready"))
        acc_ready, pos_ps, pos_read, slot_ready = (sem(n) for n in (
            "acc_ready", "pos_ps", "pos_read", "slot_ready"))
        sent = [sem(f"sent{n}") for n in range(XR)]
        dve_step, pool_step = sem("dve_step"), sem("pool_step")
        count_ps, list_ready = sem("count_ps"), sem("list_ready")
        xb_in = [sem(f"xb_in{n}") for n in range(NW)]
        ew_in = [sem(f"ew_in{n}") for n in range(NW)]
        xbT_ps, xbT_ready, gu_ps, gs_ready, hT_ready, ey_ps, ys_ready = (sem(n) for n in (
            "xbT_ps", "xbT_ready", "gu_ps", "gs_ready", "hT_ready", "ey_ps", "ys_ready"))
        put = [sem(f"put{n}") for n in range(NY)]
        sh_ps, shg_ready, shT_ready, so_ps, so_ready = (sem(n) for n in (
            "sh_ps", "shg_ready", "shT_ready", "so_ps", "so_ready"))
        pr_in = [sem(f"pr_in{n}") for n in range(NG)]
        fin_ready, stored = sem("fin_ready"), sem("stored")

        block = ctx.enter_context(nc.Block())

        NB = NEG + 1
        MORE = NOV // EG - 1
        LAST = NT + 5
        FILLS = (NE + 1) * CAP // P // FILLR
        FREST = (NE + 1) * CAP // P - FILLS * FILLR

        @block.sync
        def _(sp):
            HC = NCH // 2

            def load_group(g):
                if g >= 2:
                    sp.wait_ge(conv_ps, g - 1)
                for n in range(2):
                    if g == 0:
                        sp.dma_start(WP[:, n], wp[n]).then_inc(wp_in[n], 16)
                    sp.dma_start(X[:, g % 2, n * HC:(n + 1) * HC], xp[g, :, n * HC:(n + 1) * HC]
                                 ).then_inc(x_in[g % 2][n], 16)
                sp.dma_start(XE[:, g % 2], xe[g]).then_inc(x_in[g % 2][2], 16)

            load_group(0)
            sp.dma_start(WE[:, :, :], we.rearrange("(c k) d -> k c d", k=2 * EDGE)).then_inc(we_in, 16)
            sp.dma_start(V[:, :], vecs).then_inc(v_in, 16)
            sp.dma_start(SQ[:, :], sq).then_inc(sq_in, 16)
            sp.dma_start(C[:, :], cst).then_inc(c_in, 16)
            sp.dma_start(R[:, :], rows.partition_broadcast(P)).then_inc(r_in, 16)
            sp.dma_start(destv[:, :, :], dest.rearrange("p (t k) -> p t k", k=TOPK)).then_inc(r_in, 16)
            load_group(1)
            sp.wait_ge(filled_tile, 2)
            bufv = buf.rearrange("(p r) w -> p r w", p=P)
            for n in range(FILLS):
                if n == 3:
                    load_group(2)
                sp.dma_start(bufv[:, n * FILLR:(n + 1) * FILLR], fill[:, :, :]).then_inc(filled, 16)
            if FREST:
                sp.dma_start(bufv[:, FILLS * FILLR:], fill[:, 0:FREST]).then_inc(filled, 16)
            pairv = pair.rearrange("(p r) w -> p (r w)", p=P)
            for n in range(2):
                sp.dma_start(pairv[:, n * 2048:(n + 1) * 2048], zero[:, :]).then_inc(filled, 16)
            load_group(3)

            def load_weights(q):
                if q >= NW:
                    sp.wait_ge(ey_ps, q - NW + 1)
                sp.dma_start(w13s[:, q % NW], w13[q * EG:(q + 1) * EG].rearrange("e d n -> d e n")
                             ).then_inc(ew_in[q % NW], 16)
                sp.dma_start(w2s[HID:P, q % NW], w2[q * EG:(q + 1) * EG].rearrange("e d n -> d e n")
                             ).then_inc(ew_in[q % NW], 16)

            def load_rows(q):
                if q >= NW:
                    sp.wait_ge(ys_ready, q - NW + 1)
                    sp.wait_ge(put[(q - NW) % NY], 16 * EG * ((q - NW) // NY + 1))
                sp.dma_start(xb[:, q % NW],
                             buf[q * EG * CAP:(q + 1) * EG * CAP].rearrange("(e s) w -> s e w", e=EG)[0:BLK]
                             ).then_inc(xb_in[q % NW], 16)

            def load_overflow(n, parity):
                for e in range(EG):
                    row = sp.value_load(ovrow[0:1, bass.ds(n * EG + e, 1)], min_val=0, max_val=NE * CAP + BLK)
                    exp = sp.value_load(ovexp[0:1, bass.ds(n * EG + e, 1)], min_val=0, max_val=NE - 1)
                    sp.dma_start(xb[:, parity, e], buf[bass.ds(row, BLK), :]).then_inc(xb_in[parity], 16)
                    sp.dma_start(w13s[:, parity, e],
                                 w13[bass.ds(exp, 1)].rearrange("e d n -> (e d) n")).then_inc(ew_in[parity], 16)
                    sp.dma_start(w2s[HID:P, parity, e],
                                 w2[bass.ds(exp, 1)].rearrange("e d n -> (e d) n")).then_inc(ew_in[parity], 16)

            for q in range(NW):
                load_weights(q)
            for n in range(XR):
                sp.wait_ge(sent[n], 16 * TOPK * (NT // XR))
            for q in range(NW):
                load_rows(q)
            for q in range(NW, NEG):
                load_weights(q)
                load_rows(q)
            q = NEG
            sp.wait_ge(list_ready, 1)
            sp.wait_ge(ey_ps, q - NW + 1)
            sp.wait_ge(ys_ready, q - NW + 1)
            sp.wait_ge(put[(q - NW) % NY], 16 * EG * ((q - NW) // NY + 1))
            load_overflow(0, q % NW)
            more = sp.value_load(ovn[0:1, 0:1], min_val=0, max_val=NOV // EG - 1)
            for n in range(NY):
                sp.wait_ge(put[n], 16 * EG * len(range(n, NB, NY)))
            for n in range(MORE):
                with sp.If(more > n):
                    load_overflow(n + 1, 0)
                    sp.wait_ge(put[0], 16 * EG * (len(range(0, NB, NY)) + n + 1))
            pv = pair.rearrange("(t p k) w -> p t k w", p=P, k=TOPK)
            for g in range(NG):
                sp.dma_start(pr[:, g * TG:(g + 1) * TG], pv[:, g * TG:(g + 1) * TG]).then_inc(pr_in[g], 16)
            ov = out.rearrange("(t p) d -> p t d", p=P)
            for g in range(NG):
                sp.wait_ge(fin_ready, g + 1)
                sp.dma_start(ov[:, g * TG:(g + 1) * TG], h[:, g * TG:(g + 1) * TG]).then_inc(stored, 16)
            sp.wait_ge(stored, 16 * NG)

        @block.tensor
        def _(pe):
            HC = NCH // 2

            def conv(g, j):
                if j % HC == 0:
                    pe.wait_ge(x_in[g % 2][j // HC], 16 * (g // 2 + 1))
                    if g == 0 and j < NCH:
                        pe.wait_ge(w_ready, j // HC + 1)
                    if g == 0 and j == NCH:
                        pe.wait_ge(we_in, 16)
                if j == 0 and g >= 1:
                    pe.wait_ge(yT_ready, g)
                if j < NCH:
                    w, x = W[:, j], X[:, g % 2, j]
                else:
                    w, x = WE[:, j - NCH], XE[:, g % 2, j - NCH]
                mm = nc.tensor.matmul(CONV[:, :], w, x, start=(j == 0), stop=(j == NCH + 1))
                if j == NCH + 1:
                    mm.then_inc(conv_ps, 1)

            def embed(t):
                pe.wait_ge(yT_ready, t // TG + 1)
                if t >= 1:
                    pe.wait_ge(h_ready, t)
                y = yT[:, t // TG % 2, t % TG * P:(t % TG + 1) * P]
                nc.tensor.transpose(A[:, 0:P], y, ident)
                nc.tensor.matmul(A[:, P:2 * P], y, WD[:, :], start=True, stop=True).then_inc(y_ps, 1)

            def turn_xn(t):
                pe.wait_ge(xn_ready, t + 1)
                if t >= 4:
                    pe.wait_ge(x2T_ready, t - 3)
                nc.tensor.transpose(TR[:, 0:P], xn[:, t % 2], ident).then_inc(xnT_ps, 1)

            def project(t):
                pe.wait_ge(xnT_ready, t + 1)
                if t >= 1:
                    pe.wait_ge(qk_ready, t)
                nc.tensor.matmul(QK[:, 0:P], wq, xnT[:, t % 2], start=True, stop=True)
                nc.tensor.matmul(QK[:, P:2 * P], wk, xnT[:, t % 2], start=True, stop=True).then_inc(qk_ps, 1)
                if t >= 1:
                    pe.wait_ge(vg_ready, t)
                nc.tensor.matmul(VG[:, 0:2 * P], xnT[:, t % 2], wvg, start=True, stop=True).then_inc(vg_ps, 1)

            def scores(t):
                pe.wait_ge(qk_ready, t + 1)
                if t >= 1:
                    pe.wait_ge(st_ready, t)
                half = P // 2
                for n, s in enumerate((S0, S1)):
                    mm = nc.tensor.matmul(s[:, :], kT[n * half:(n + 1) * half, t % 2],
                                          qm[n * half:(n + 1) * half, t % 2].rearrange("p a i -> p (a i)"),
                                          start=True, stop=True)
                mm.then_inc(s_ps, 1)

            def attend(t):
                pe.wait_ge(st_ready, t + 1)
                pe.wait_ge(vg_ready, t + 1)
                if t >= 2:
                    pe.wait_ge(th_ready, t - 1)
                for hh in range(HEADS):
                    mm = nc.tensor.matmul(O[:, hh * HD:(hh + 1) * HD], ST[:, t % 2, hh],
                                          vg[:, t % 4, hh * HD:(hh + 1) * HD], start=True, stop=True)
                mm.then_inc(av_ps, 1)

            def places(t):
                pe.wait_ge(oh_ready, t + 1)
                if t == 0:
                    pe.wait_ge(before_ready, 1)
                    pe.wait_ge(ones_set, 1)
                if t >= 1:
                    pe.wait_ge(acc_ready, t)
                pe.wait_ge(av_read, min(t + 3, NT))
                pe.wait_ge(th_ready, t + 1)
                for k in range(TOPK):
                    mm = nc.tensor.matmul(O[:, 0:NE], before[:, :], OH[:, t % 4, k],
                                          start=(k == 0), stop=(t == 0 and k == TOPK - 1))
                if t >= 1:
                    mm = nc.tensor.matmul(O[:, 0:NE], ones[:, :], acc[:, t % 3], start=False, stop=True)
                mm.then_inc(pos_ps, 1)

            def turn_xf(t):
                pe.wait_ge(xf_ready, t + 1)
                pe.wait_ge(xnT_ready, min(t + 4, NT))
                nc.tensor.transpose(TR[:, 0:P], xrow[:, t % XR, 0, 0:P], ident).then_inc(x2T_ps, 1)

            def logits(t):
                pe.wait_ge(x2T_ready, t + 1)
                if t >= 1:
                    pe.wait_ge(pos_read, t)
                pe.wait_ge(av_read, min(t + 2, NT))
                nc.tensor.matmul(O[:, 0:NE], x2T[:, t], gw, start=True, stop=True).then_inc(lg_ps, 1)

            for j in range(NCH + 2):
                conv(0, j)
            pe.wait_ge(c_in, 16)
            pe.wait_ge(sq_in, 16)
            pe.wait_ge(wd_in_ready, 1)
            nc.tensor.matmul(QK[:, 0:P], center, gdw[:, :], start=True, stop=True)
            nc.tensor.matmul(VG[:, 0:P], betab[:, :], dw, start=True, stop=True).then_inc(wd_ps, 1)
            pe.wait_ge(wd_ready, 1)
            pe.wait_ge(cvec_ready, 1)
            CHUNKS = (range(0, 3), range(3, 6), range(6, 8), range(0))
            for i in range(LAST):
                if i < NT:
                    embed(i)
                if 0 <= i - 1 < NT:
                    turn_xn(i - 1)
                if 0 <= i - 3 < NT:
                    attend(i - 3)
                if 0 <= i - 1 < NT:
                    project(i - 1)
                if 0 <= i - 4 < NT:
                    turn_xf(i - 4)
                if 0 <= i - 2 < NT:
                    scores(i - 2)
                if 0 <= i - 5 < NT:
                    places(i - 5)
                if i // TG + 1 < NG:
                    for j in CHUNKS[i % TG]:
                        conv(i // TG + 1, j)
                if 0 <= i - 4 < NT:
                    logits(i - 4)
            pe.wait_ge(acc_ready, NT)
            pe.wait_ge(pos_read, NT)
            nc.tensor.matmul(O[:, 0:NE], ones[:, :], acc[:, NT % 3], start=True, stop=True).then_inc(count_ps, 1)

            def turn_rows(q, u, v=0, first=False, back=2):
                if not first:
                    pe.wait_ge(xbT_ready, q - back + 1)
                for e in range(EG):
                    mm = nc.tensor.transpose(XT[u][:, e * BLK:(e + 1) * BLK], xb[:, v, e, 0:P], ident)
                mm.then_inc(xbT_ps, 1)

            def gate_up(q, u, v=0, first=False, back=2):
                if not first:
                    pe.wait_ge(hT_ready, q - back + 1)
                pe.wait_ge(xbT_ready, q + 1)
                for e in range(EG):
                    mm = nc.tensor.matmul(GU[u][:, e * BLK:(e + 1) * BLK], w13s[:, v, e], xbT[:, u, e],
                                          start=True, stop=True)
                mm.then_inc(gu_ps, 1)

            def down(q, u, v=0, first=False, back=2):
                if not first:
                    pe.wait_ge(ys_ready, q - back + 1)
                pe.wait_ge(hT_ready, q + 1)
                for e in range(EG):
                    mm = nc.tensor.matmul(Y[u][:, e * P:(e + 1) * P], hT[HID:P, u, e], w2s[HID:P, v, e],
                                          start=True, stop=True)
                mm.then_inc(ey_ps, 1)

            def shared_up(g):
                if g == 0:
                    pe.wait_ge(x2T_ready, NT)
                    pe.wait_ge(st_ready, NT)
                    pe.wait_ge(list_ready, 1)
                else:
                    pe.wait_ge(so_ready, g)
                x = x2T[:, g * TG:(g + 1) * TG].rearrange("p t n -> p (t n)")
                nc.tensor.matmul(SH1[:, :], s1, x, start=True, stop=True)
                nc.tensor.matmul(SH3[:, :], s3, x, start=True, stop=True).then_inc(sh_ps, 1)

            def shared_down(g):
                pe.wait_ge(shT_ready, g + 1)
                for n in range(TG):
                    mm = nc.tensor.matmul(SH1[:, n * P:(n + 1) * P], shT[:, n], s2, start=True, stop=True)
                mm.then_inc(so_ps, 1)

            shared_up(0)
            shared_down(0)
            for i in range(NB + 2):
                if i < NB:
                    pe.wait_ge(xb_in[i % NW], 16 * (i // NW) + (16 if i < NEG else 16 * EG))
                    turn_rows(i, i % 2, i % NW, first=i < 2)
                if 0 <= i - 1 < NB:
                    q = i - 1
                    pe.wait_ge(ew_in[q % NW], 32 * (q // NW) + (32 if q < NEG else 32 * EG))
                    gate_up(q, q % 2, q % NW, first=q < 2)
                if 0 <= i - 2 < NB:
                    down(i - 2, (i - 2) % 2, (i - 2) % NW, first=i - 2 < 2)
                if i in (3, 6, 9):
                    shared_up(i // 3)
                if i in (4, 7, 10):
                    shared_down(i // 3)
            more = pe.value_load(ovn[0:1, 0:1], min_val=0, max_val=NOV // EG - 1)
            for n in range(MORE):
                with pe.If(more > n):
                    pe.wait_ge(xb_in[0], 16 * len(range(0, NEG, NW)) + (n + 1) * 16 * EG)
                    pe.wait_ge(ew_in[0], 32 * len(range(0, NEG, NW)) + (n + 1) * 32 * EG)
                    turn_rows(n + NB, 0, back=1)
                    gate_up(n + NB, 0, back=1)
                    down(n + NB, 0, back=1)

        @block.scalar
        def _(act):
            def evac_y(g):
                act.wait_ge(conv_ps, g + 1)
                if g == 0:
                    act.wait_ge(v_in, 16)
                if g >= 2:
                    act.wait_ge(y_ps, TG * (g - 1))
                nc.scalar.activation(yT[:, g % 2].rearrange("d (b p) -> d b p", p=T),
                                     CONV[:, :].rearrange("d (p b) -> d b p", p=T),
                                     ACT.Identity, bias=conv_b).then_inc(yT_ready, 1)

            def evac_xn(t):
                act.wait_ge(xnT_ps, t + 1)
                if t >= 2:
                    act.wait_ge(vg_ps, t - 1)
                nc.scalar.activation(xnT[:, t % 2], TR[:, 0:P], ACT.Copy).then_inc(xnT_ready, 1)

            def evac_qk(t):
                act.wait_ge(qk_ps, t + 1)
                if t == 0:
                    act.wait_ge(bqm_ready, 1)
                if t >= 2:
                    act.wait_ge(s_ps, t - 1)
                for m in range(QM):
                    nc.scalar.activation(qm[:, t % 2, m], QK[:, 0:P], ACT.Identity,
                                         bias=bqm[:, m:m + 1], scale=head[:, m:m + 1])
                nc.scalar.activation(kT[:, t % 2], QK[:, P:2 * P], ACT.Identity, bias=bk).then_inc(qk_ready, 1)

            def gates(t):
                act.wait_ge(vg_ready, t + 1)
                nc.scalar.activation(vg[:, t % 4, P:2 * P], vg[:, t % 4, P:2 * P], ACT.Silu).then_inc(g_ready, 1)

            def evac_xf(t):
                act.wait_ge(x2T_ps, t + 1)
                nc.scalar.activation(x2T[:, t], TR[:, 0:P], ACT.Copy).then_inc(x2T_ready, 1)

            def tanhs(t):
                act.wait_ge(lg_ps, t + 1)
                if t >= 2:
                    act.wait_ge(oh_ready, t - 1)
                nc.scalar.activation(th[:, t % 2], O[:, 0:NE], ACT.Tanh, scale=0.5).then_inc(th_ready, 1)

            evac_y(0)
            act.wait_ge(wd_ps, 1)
            nc.scalar.activation(WD[:, :], QK[:, 0:P], ACT.Copy).then_inc(wd_ready, 1)
            for i in range(LAST):
                if 0 <= i - 1 < NT:
                    evac_xn(i - 1)
                    evac_qk(i - 1)
                if 0 <= i - 4 < NT:
                    evac_xf(i - 4)
                if 0 <= i - 1 < NT:
                    gates(i - 1)
                if 0 <= i - 4 < NT:
                    tanhs(i - 4)
                if i % TG == 2 and i // TG + 1 < NG:
                    evac_y(i // TG + 1)

            def evac_rows(q, u, v=0, first=False, back=2):
                act.wait_ge(xbT_ps, q + 1)
                if not first:
                    act.wait_ge(gu_ps, q - back + 1)
                nc.scalar.activation(xbT[:, u].rearrange("p e s -> p (e s)"), XT[u][:, :], ACT.Copy
                                     ).then_inc(xbT_ready, 1)

            def gate(q, u, v=0, first=False, back=2):
                act.wait_ge(gu_ps, q + 1)
                if not first:
                    act.wait_ge(hT_ready, q - back + 1)
                nc.scalar.activation(gs[HID:P, u], GU[u][0:HID, :], ACT.Silu).then_inc(gs_ready, 1)

            def shared_gate(g):
                act.wait_ge(sh_ps, g + 1)
                if g >= 1:
                    act.wait_ge(shT_ready, g)
                nc.scalar.activation(shg[:, :], SH1[:, :], ACT.Silu).then_inc(shg_ready, 1)

            shared_gate(0)
            for i in range(NB + 1):
                if i < NB:
                    evac_rows(i, i % 2, first=i < 2)
                if 0 <= i - 1 < NB:
                    gate(i - 1, (i - 1) % 2, first=i - 1 < 2)
                if i in (3, 6, 9):
                    shared_gate(i // 3)
            more = act.value_load(ovn[0:1, 0:1], min_val=0, max_val=NOV // EG - 1)
            for n in range(MORE):
                with act.If(more > n):
                    evac_rows(n + NB, 0, back=1)
                    gate(n + NB, 0, back=1)

        @block.vector
        def _(dve):
            steps = [0]

            def own(ins):
                steps[0] += 1
                ins.then_inc(dve_step, 1)
                dve.wait_ge(dve_step, steps[0])

            HC = NCH // 2
            for n in range(2):
                dve.wait_ge(wp_in[n], 16)
                c = slice(n * HC, (n + 1) * HC)
                own(nc.vector.tensor_tensor(W[:, c], WP[:, n, 0], WP[:, n, 1], ALU.add))
                for s in range(2, 5):
                    ins = nc.vector.tensor_tensor(W[:, c], W[:, c], WP[:, n, s], ALU.add)
                    if s == 4:
                        ins.then_inc(w_ready, 1)
                    else:
                        own(ins)
            dve.wait_ge(v_in, 16)
            dve.wait_ge(sq_in, 16)
            nc.vector.tensor_scalar(gdw[:, :], dw, gamma, None, ALU.mult)
            nc.vector.tensor_copy(betab[:, :], beta.to_broadcast([P, P])).then_inc(wd_in_ready, 1)
            dve.wait_ge(c_in, 16)
            nc.vector.tensor_copy(before[:, :], before_f).then_inc(before_ready, 1)
            nc.vector.tensor_scalar(bqm[:, :], head, bq, None, ALU.mult).then_inc(bqm_ready, 1)
            dve.wait_ge(r_in, 32)
            dve.wait_ge(wd_ps, 1)
            nc.vector.tensor_tensor(cvec[:, :], VG[:, 0:P], dense_bias, ALU.add).then_inc(cvec_ready, 1)

            def stats_y(t):
                dve.wait_ge(y_ps, t + 1)
                own(nc.vector.bn_stats(st1[:, t % 2], A[:, 0:P]))
                nc.vector.bn_aggr(mv1[:, t % 2], st1[:, t % 2]).then_inc(ystat, 1)

            def make_h(t):
                dve.wait_ge(r1_ready, t + 1)
                if t == 0:
                    dve.wait_ge(cvec_ready, 1)
                nc.vector.scalar_tensor_tensor(out=h[:, t], in0=A[:, P:2 * P], scalar=rs1[:, t % 2],
                                               in1=cvec[:, :], op0=ALU.mult, op1=ALU.add).then_inc(h_ready, 1)
                dve.wait_ge(h_ready, t + 1)
                own(nc.vector.bn_stats(st2[:, t % 2], h[:, t]))
                nc.vector.bn_aggr(mv2[:, t % 2], st2[:, t % 2]).then_inc(hstat, 1)

            def norm_h(t):
                dve.wait_ge(r2_ready, t + 1)
                if t >= 2:
                    dve.wait_ge(xnT_ps, t - 1)
                nc.vector.tensor_scalar(xn[:, t % 2], h[:, t], mv2[:, t % 2, 0:1], rs2[:, t % 2],
                                        ALU.subtract, ALU.mult).then_inc(xn_ready, 1)

            def bias_vg(t):
                dve.wait_ge(vg_ps, t + 1)
                if t >= 4:
                    dve.wait_ge(av_ps, t - 3)
                nc.vector.tensor_tensor(vg[:, t % 4], VG[:, 0:2 * P], vg_bias, ALU.add).then_inc(vg_ready, 1)

            def decay_scores(t):
                dve.wait_ge(s_ps, t + 1)
                if t >= 2:
                    dve.wait_ge(av_ps, t - 1)
                for n, s in enumerate((S0, S1)):
                    ins = nc.vector.tensor_tensor(
                        ST[:, t % 2, n * QM:(n + 1) * QM].rearrange("p a i -> p (a i)"), s[:, :],
                        decay[:, n * 512:(n + 1) * 512], ALU.mult)
                ins.then_inc(st_ready, 1)

            def add_attention(t):
                dve.wait_ge(av_ps, t + 1)
                dve.wait_ge(g_ready, t + 1)
                nc.vector.tensor_tensor(go[:, :], O[:, 0:P], vg[:, t % 4, P:2 * P], ALU.mult).then_inc(av_read, 1)
                dve.wait_ge(av_read, t + 1)
                nc.vector.tensor_tensor(h[:, t], h[:, t], go[:, :], ALU.add).then_inc(h2_ready, 1)
                dve.wait_ge(h2_ready, t + 1)
                own(nc.vector.bn_stats(st3[:, t % 2], h[:, t]))
                nc.vector.bn_aggr(mv3[:, t % 2], st3[:, t % 2]).then_inc(h2stat, 1)

            def norm_h2(t):
                dve.wait_ge(r3_ready, t + 1)
                if t >= XR:
                    dve.wait_ge(sent[t % XR], 16 * TOPK * (t // XR))
                    dve.wait_ge(x2T_ps, t - XR + 1)
                nc.vector.tensor_scalar(xrow[:, t % XR, :, 0:P], h[:, t:t + 1].broadcast_to([P, TOPK, P]),
                                        mv3[:, t % 2, 0:1], rs3[:, t % 2],
                                        ALU.subtract, ALU.mult).then_inc(xf_ready, 1)

            def choose(t):
                dve.wait_ge(th_ready, t + 1)
                own(nc.vector.tensor_scalar(sg[:, :], th[:, t % 2], 0.5, 0.5, ALU.mult, ALU.add))
                own(nc.vector.max(top[:, :], sg[:, :]))
                own(nc.vector.max_index(topi[:, :], top[:, :], sg[:, :]))
                own(nc.vector.tensor_copy(idx[:, t % 4], topi[:, 0:TOPK]))
                if t >= 4:
                    dve.wait_ge(pos_ps, t - 3)
                    dve.wait_ge(acc_ready, t - 3)
                nc.vector.tensor_tensor(OH[:, t % 4], expert.unsqueeze(1).broadcast_to([P, TOPK, NE]),
                                        idx[:, t % 4].unsqueeze(2).broadcast_to([P, TOPK, NE]),
                                        ALU.is_equal).then_inc(oh_ready, 1)
                own(nc.vector.tensor_scalar(ssum[:, :], top[:, 0:1], top[:, 1:2], 1e-20, ALU.add, ALU.add))
                own(nc.vector.reciprocal(srec[:, :], ssum[:, :]))
                nc.vector.tensor_scalar(xrow[:, t % XR, :, P], top[:, 0:TOPK], srec[:, 0:1], ROUTE_SCALE,
                                        ALU.mult, ALU.mult)
                nc.vector.tensor_copy(xrow[:, t % XR, :, P + 1].bitcast(I32), destv[:, t]).then_inc(meta_ready, 1)

            def find_slots(t):
                dve.wait_ge(pos_ps, t + 1)
                nc.vector.tensor_tensor(mpos[:, :, :], O[:, 0:NE].unsqueeze(1).broadcast_to([P, TOPK, NE]),
                                        OH[:, t % 4], ALU.mult).then_inc(pos_read, 1)
                dve.wait_ge(pos_read, t + 1)
                own(nc.vector.tensor_reduce(pos[:, :], mpos[:, :, :], AX.X, ALU.add))
                own(nc.vector.tensor_scalar(over[:, :], pos[:, :], CAP - 0.5, float(BIG), ALU.is_gt, ALU.mult))
                own(nc.vector.tensor_tensor(place[:, :], over[:, :], pos[:, :], ALU.add))
                nc.vector.scalar_tensor_tensor(out=slots[:, :, t], in0=idx[:, t % 4], scalar=float(CAP),
                                               in1=place[:, :], op0=ALU.mult, op1=ALU.add).then_inc(slot_ready, 1)

            for i in range(LAST):
                if i < NT:
                    stats_y(i)
                if 0 <= i - 5 < NT:
                    choose(i - 5)
                if 0 <= i - 3 < NT:
                    add_attention(i - 3)
                if i < NT:
                    make_h(i)
                if 0 <= i - 1 < NT:
                    bias_vg(i - 1)
                if 0 <= i - 2 < NT:
                    decay_scores(i - 2)
                if 0 <= i - 5 < NT:
                    find_slots(i - 5)
                if i < NT:
                    norm_h(i)
                if 0 <= i - 3 < NT:
                    norm_h2(i - 3)

            dve.wait_ge(count_ps, 1)
            own(nc.vector.scalar_tensor_tensor(out=ovv[:, :], in0=O[:, 0:NE], scalar=BLK + 0.5, in1=left,
                                               op0=ALU.is_gt, op1=ALU.mult))
            for n in range(NOV // 8):
                src, dst = (ovv, ovw) if n % 2 == 0 else (ovw, ovv)
                own(nc.vector.max(ovl[:, 8 * n:8 * n + 8], src[:, :]))
                if n < NOV // 8 - 1:
                    own(nc.vector.match_replace(dst[:, :], ovl[:, 8 * n:8 * n + 8], src[:, :], 0.0))
            own(nc.vector.tensor_scalar(ovf[:, :], ovl[:, :], -1.0, float(NE), ALU.mult, ALU.add))
            nc.vector.tensor_scalar(ovrow[:, :], ovf[:, :], float(CAP), float(BLK), ALU.mult, ALU.add)
            nc.vector.tensor_scalar(ovexp[:, :], ovf[:, :], float(NE - 1), None, ALU.min)
            own(nc.vector.tensor_scalar(ovc[:, :], ovl[:, ::EG], 0.5, None, ALU.is_gt))
            own(nc.vector.tensor_reduce(ovs[:, :], ovc[:, 1:], AX.X, ALU.add))
            nc.vector.tensor_copy(ovn[:, :], ovs[:, :]).then_inc(list_ready, 1)

            def hidden(q, u, v=0, first=False, back=2):
                dve.wait_ge(gs_ready, q + 1)
                if not first:
                    dve.wait_ge(ey_ps, q - back + 1)
                nc.vector.tensor_tensor(hT[HID:P, u].rearrange("p e s -> p (e s)"), GU[u][HID:P, :],
                                        gs[HID:P, u], ALU.mult).then_inc(hT_ready, 1)

            def weigh(q, u, v=0, first=False, back=2):
                dve.wait_ge(ey_ps, q + 1)
                z = q % NY if q < NB else 0
                if q >= NY:
                    dve.wait_ge(put[z], 16 * EG * (q // NY if q < NB else q - NB + len(range(0, NB, NY))))
                nc.vector.tensor_tensor(ys[:, z], Y[u][:, :].rearrange("p (e n) -> p e n", e=EG),
                                        xb[:, v, :, P:P + 1].broadcast_to([P, EG, P]),
                                        ALU.mult).then_inc(ys_ready, 1)

            def shared_hidden(g):
                dve.wait_ge(shg_ready, g + 1)
                if g >= 1:
                    dve.wait_ge(so_ps, g)
                nc.vector.tensor_tensor(shT[:, :].rearrange("p t n -> p (t n)"), SH3[:, :], shg[:, :],
                                        ALU.mult).then_inc(shT_ready, 1)

            def shared_add(g):
                dve.wait_ge(so_ps, g + 1)
                hg = h[:, g * TG:(g + 1) * TG].rearrange("p t n -> p (t n)")
                nc.vector.tensor_tensor(hg, SH1[:, :], hg, ALU.add).then_inc(so_ready, 1)

            shared_hidden(0)
            shared_add(0)
            for i in range(NB + 2):
                if 0 <= i - 1 < NB:
                    hidden(i - 1, (i - 1) % 2, first=i - 1 < 2)
                if 0 <= i - 2 < NB:
                    weigh(i - 2, (i - 2) % 2, (i - 2) % NW, first=i - 2 < 2)
                if i in (3, 6, 9):
                    shared_hidden(i // 3)
                if i in (4, 7, 10):
                    shared_add(i // 3)
            more = dve.value_load(ovn[0:1, 0:1], min_val=0, max_val=NOV // EG - 1)
            for n in range(MORE):
                with dve.If(more > n):
                    hidden(n + NB, 0, back=1)
                    weigh(n + NB, 0, back=1)

            for g in range(NG):
                dve.wait_ge(pr_in[g], 16)
                dve.wait_ge(so_ready, g + 1)
                t = slice(g * TG, (g + 1) * TG)
                own(nc.vector.tensor_tensor(h[:, t], h[:, t], pr[:, t, 0], ALU.add))
                nc.vector.tensor_tensor(h[:, t], h[:, t], pr[:, t, 1], ALU.add).then_inc(fin_ready, 1)

        @block.gpsimd
        def _(pool):
            steps = [0]

            def own(ins):
                steps[0] += 1
                ins.then_inc(pool_step, 1)
                pool.wait_ge(pool_step, steps[0])

            own(pool.memset(fill[:, :, :], 0.0))
            pool.memset(fill[:, :, P + 1:P + 2].bitcast(I32), BIG).then_inc(filled_tile, 1)
            pool.memset(zero[:, :], 0.0).then_inc(filled_tile, 1)
            pool.memset(mhalf[:, :], -0.5)
            pool.memset(acc[:, 0], 0.0)
            own(pool.memset(ones[:, :], 1.0))
            pool.sem_inc(ones_set, 1)

            def rstd(t, stat, eps, mv, ve, rs, ready):
                pool.wait_ge(stat, t + 1)
                own(pool.tensor_scalar(ve[:, t % 2], mv[:, t % 2, 1:2], 1.0, eps, ALU.mult, ALU.add))
                pool.tensor_tensor(rs[:, t % 2], ve[:, t % 2], mhalf[:, :], ALU.pow).then_inc(ready, 1)

            def accumulate(t):
                pool.wait_ge(oh_ready, t + 1)
                if t >= 2:
                    pool.wait_ge(pos_ps, t - 1)
                own(pool.tensor_tensor(acc[:, (t + 1) % 3], acc[:, t % 3], OH[:, t % 4, 0], ALU.add))
                pool.tensor_tensor(acc[:, (t + 1) % 3], acc[:, (t + 1) % 3], OH[:, t % 4, 1], ALU.add
                                   ).then_inc(acc_ready, 1)
                pool.wait_ge(acc_ready, t + 1)

            def send(t):
                pool.wait_ge(slot_ready, t + 1)
                pool.wait_ge(meta_ready, t + 1)
                if t == 0:
                    pool.wait_ge(filled, 16 * (FILLS + (FREST > 0) + 2))
                for k in range(TOPK):
                    pool.indirect_dma_start(
                        buf, bass.IndirectOffsetOnAxis(ap=slots[:, k, t:t + 1], axis=0),
                        xrow[:, t % XR, k], None, bounds_check=NE * CAP - 1, oob_is_err=False
                    ).then_inc(sent[t % XR], 16)

            to_send = 0
            for i in range(LAST):
                if i < NT:
                    rstd(i, ystat, LN_TOK, mv1, ve1, rs1, r1_ready)
                if 0 <= i - 3 < NT:
                    rstd(i - 3, h2stat, LN, mv3, ve3, rs3, r3_ready)
                if i < NT:
                    rstd(i, hstat, LN, mv2, ve2, rs2, r2_ready)
                if 0 <= i - 5 < NT:
                    accumulate(i - 5)
                while i >= 7 and to_send < min(i - 4, NT) and (i >= 12 or to_send <= i - 7):
                    send(to_send)
                    to_send += 1

            assert to_send == NT

            def scatter(q, z, v):
                pool.wait_ge(ys_ready, q + 1)
                for e in range(EG):
                    pool.indirect_dma_start(
                        pair, bass.IndirectOffsetOnAxis(ap=xb[:, v, e, P + 1:P + 2].bitcast(U32), axis=0),
                        ys[:, z, e], None, bounds_check=TOKENS * TOPK - 1, oob_is_err=False
                    ).then_inc(put[z], 16)

            for q in range(NB):
                scatter(q, q % NY, q % NW)
            more = pool.value_load(ovn[0:1, 0:1], min_val=0, max_val=NOV // EG - 1)
            for n in range(MORE):
                with pool.If(more > n):
                    scatter(n + NB, 0, 0)


def kernel(x, L0_tok_conv_w, L0_tok_conv_b, L0_tok_gamma, L0_tok_beta, L0_tok_dense_w, L0_tok_dense_b,
           L0_attn_wq, L0_attn_bq, L0_attn_wk, L0_attn_bk, L0_attn_wv, L0_attn_bv, L0_attn_wg, L0_attn_bg,
           L0_ffn_gate_w, L0_ffn_w1, L0_ffn_w3, L0_ffn_w2, L0_ffn_sw1, L0_ffn_sw3, L0_ffn_sw2):
    import concourse.bacc as bacc
    from concourse.bass_utils import run_bass_kernel_spmd

    x = np.asarray(x)
    img = x.reshape(NG, GB, GRID, PATCH, GRID, PATCH, CH).transpose(0, 3, 5, 6, 2, 4, 1)
    xp = np.ascontiguousarray(img).reshape(NG, NCH, P, GN).transpose(0, 2, 1, 3)
    xe = np.zeros((NG, 4, EDGE, GRID, GRID, GB), x.dtype)
    xe[:, 0, :, 1:] = img[:, PATCH - 1].reshape(NG, EDGE, GRID, GRID, GB)[:, :, :-1]
    xe[:, 1, :, :-1] = img[:, 0].reshape(NG, EDGE, GRID, GRID, GB)[:, :, 1:]
    xe[:, 2, :, :, 1:] = img[:, :, PATCH - 1].reshape(NG, EDGE, GRID, GRID, GB)[:, :, :, :-1]
    xe[:, 3, :, :, :-1] = img[:, :, 0].reshape(NG, EDGE, GRID, GRID, GB)[:, :, :, 1:]
    xe = xe.reshape(NG, 2, 2 * EDGE, GN).transpose(0, 2, 1, 3)

    cw = np.asarray(L0_tok_conv_w).reshape(PATCH, PATCH, 5, CH, P)
    wp = np.zeros((5, PATCH, PATCH, CH, P), cw.dtype)
    wp[0] = cw[:, :, 0]
    wp[1, :, :-1] = cw[:, 1:, 1]
    wp[2, :, 1:] = cw[:, :-1, 2]
    wp[3, :-1] = cw[1:, :, 3]
    wp[4, 1:] = cw[:-1, :, 4]
    wp = wp.reshape(5, 2, NCH // 2, P, P).transpose(1, 3, 0, 2, 4)
    we = np.concatenate([cw[0, :, 3].reshape(EDGE, P), cw[PATCH - 1, :, 4].reshape(EDGE, P),
                         cw[:, 0, 1].reshape(EDGE, P), cw[:, PATCH - 1, 2].reshape(EDGE, P)])

    sq = np.concatenate([np.asarray(L0_tok_dense_w), np.asarray(L0_attn_wq).T, np.asarray(L0_attn_wk).T,
                         np.asarray(L0_attn_wv).T, np.asarray(L0_attn_wg).T, np.asarray(L0_ffn_sw1),
                         np.asarray(L0_ffn_sw3), np.asarray(L0_ffn_sw2), np.asarray(L0_ffn_gate_w).T], 1)
    w13 = np.concatenate([np.asarray(L0_ffn_w1), np.asarray(L0_ffn_w3)], 2)
    vecs = np.stack([np.asarray(v) for v in (L0_tok_conv_b, L0_tok_gamma, L0_tok_beta, L0_attn_bq, L0_attn_bk)], 1)
    rows = np.concatenate([np.asarray(L0_attn_bv), np.asarray(L0_attn_bg), np.asarray(L0_tok_dense_b)])
    cst, dest = constants()

    nc = bacc.Bacc("TRN2", target_bir_lowering=False, num_devices=1)
    arrays, args = {}, []
    for name, a in (("xp", xp), ("xe", xe), ("wp", wp), ("we", we), ("sq", sq), ("w13", w13),
                    ("w2", np.asarray(L0_ffn_w2)), ("vecs", vecs), ("rows", rows), ("cst", cst), ("dest", dest)):
        a = np.ascontiguousarray(a)
        arrays[name] = a
        args.append(nc.dram_tensor(name, a.shape, mybir.dt.from_np(a.dtype), kind="ExternalInput").ap())
    res = nc.dram_tensor("out", (TOKENS, P), F32, kind="ExternalOutput").ap()
    tower(nc, *args, res)
    r = run_bass_kernel_spmd(nc, [arrays], core_ids=[0])
    return np.asarray(r.results[0]["out"]).reshape(IMAGES, T, P)
```

```python
from contextlib import ExitStack

import numpy as np

import concourse.bass as bass
from concourse import mybir

F32 = mybir.dt.float32
BF16 = mybir.dt.bfloat16
I32 = mybir.dt.int32
U32 = mybir.dt.uint32
ALU = mybir.AluOpType
ACT = mybir.ActivationFunctionType
AX = mybir.AxisListType

P = 128
IMAGES, SIDE, CH = 128, 64, 3
PATCH = 16
GRID = SIDE // PATCH
T = GRID * GRID
TOKENS = IMAGES * T
NT = TOKENS // P
TG = 4
NG = NT // TG
GN = TG * P
GB = IMAGES // NG
KP = PATCH * PATCH * CH
NCH = KP // P
EDGE = PATCH * CH
HEADS = 8
HD = P // HEADS
QM = 4
NE = 64
TOPK = 2
CAP = 256
HID = 64
BLK = 128
EG = 4
NEG = NE // EG
NOV = 32
ROW = P + 2
BIG = 1 << 20
LN_TOK, LN = 1e-3, 1e-5
ROUTE_SCALE = 2.5
assert (TOKENS * TOPK) // (BLK + 1) < NOV


def constants():
    ident = np.eye(P, dtype=np.float32)
    center = ident - np.float32(1.0 / P)
    gam = (1.0 - 2.0 ** (-5.0 - np.arange(HEADS, dtype=np.float32))).astype(np.float32)
    j, i = np.arange(P)[:, None], np.arange(P)[None, :]
    keep = (j // T == i // T) & (j >= i)
    decay = np.zeros((P, HEADS, P), np.float32)
    for h in range(HEADS):
        decay[:, h] = np.where(keep, gam[h] ** np.maximum(j - i, 0).astype(np.float32), 0.0)
    decay *= np.float32(HD ** -0.5)
    before = (j < i).astype(np.float32)
    expert = np.broadcast_to(np.arange(NE, dtype=np.float32), (P, NE))
    left = np.broadcast_to(NE - np.arange(NE, dtype=np.float32), (P, NE))
    head = (np.arange(P)[:, None] // HD % QM == np.arange(QM)[None, :]).astype(np.float32)
    flat = np.concatenate([ident, center, before, expert, left, head, decay.reshape(P, -1)], 1)
    token = np.arange(NT)[None, :, None] * P + np.arange(P)[:, None, None]
    dest = (token * TOPK + np.arange(TOPK)[None, None, :]).astype(np.int32).reshape(P, NT * TOPK)
    return np.ascontiguousarray(flat, np.float32), np.ascontiguousarray(dest)


NC_CONST = 3 * P + 2 * NE + QM + HEADS * P


def tower(nc, xp, xe, wp, we, sq, w13, w2, vecs, rows, cst, dest, out):
    ctx = ExitStack()
    with ctx:
        def sb(name, shape, dt=F32):
            return ctx.enter_context(nc.sbuf_tensor(name, shape, dt))

        def sem(name):
            return ctx.enter_context(nc.semaphore(name))

        buf = nc.dram_tensor("expert_rows", ((NE + 1) * CAP, ROW), F32, kind="Internal").ap()
        pair = nc.dram_tensor("pair_rows", (TOKENS * TOPK, P), F32, kind="Internal").ap()

        C = sb("C", [P, NC_CONST])
        ident = C[:, 0:P]
        center = C[:, P:2 * P]
        before_f = C[:, 2 * P:3 * P]
        expert = C[:, 3 * P:3 * P + NE]
        left = C[:, 3 * P + NE:3 * P + 2 * NE]
        head = C[:, 3 * P + 2 * NE:3 * P + 2 * NE + QM]
        decay = C[:, 3 * P + 2 * NE + QM:NC_CONST]
        destv = sb("destv", [P, NT, TOPK], I32)
        V = sb("V", [P, 5])
        conv_b, gamma, beta, bq, bk = (V[:, n:n + 1] for n in range(5))
        R = sb("R", [P, 3 * P])
        vg_bias, dense_bias = R[:, 0:2 * P], R[:, 2 * P:3 * P]
        SQ = sb("SQ", [P, 8 * P + NE])
        dw, wq, wk, wvg, s1, s3, s2, gw = (SQ[:, a:b] for a, b in (
            (0, P), (P, 2 * P), (2 * P, 3 * P), (3 * P, 5 * P), (5 * P, 6 * P), (6 * P, 7 * P),
            (7 * P, 8 * P), (8 * P, 8 * P + NE)))
        WP = sb("WP", [P, 2, 5, NCH // 2, P])
        W = sb("W", [P, NCH, P])
        WE = sb("WE", [2 * EDGE, 2, P])
        gdw = sb("gdw", [P, P])
        WD = sb("WD", [P, P])
        betab = sb("betab", [P, P])
        cvec = sb("cvec", [P, P])
        bqm = sb("bqm", [P, QM])
        before = sb("before", [P, P], BF16)
        ones = sb("ones", [P, P], BF16)
        mhalf = sb("mhalf", [P, 1])
        FILLR = 16
        fill = sb("fill", [P, FILLR, ROW])
        zero = sb("zero", [P, 2048])

        XR = 8
        X = sb("X", [P, 2, NCH, GN])
        XE = sb("XE", [2 * EDGE, 2, 2, GN])
        yT = sb("yT", [P, 2, GN])
        h = sb("h", [P, NT, P])
        x2T = sb("x2T", [P, NT, P])
        st1, st2, st3 = (sb(f"st{n}", [P, 2, 6]) for n in (1, 2, 3))
        mv1, mv2, mv3 = (sb(f"mv{n}", [P, 2, 2]) for n in (1, 2, 3))
        ve1, ve2, ve3 = (sb(f"ve{n}", [P, 2, 1]) for n in (1, 2, 3))
        rs1, rs2, rs3 = (sb(f"rs{n}", [P, 2, 1]) for n in (1, 2, 3))
        xn = sb("xn", [P, 2, P])
        xnT = sb("xnT", [P, 2, P])
        qm = sb("qm", [P, 2, QM, P])
        kT = sb("kT", [P, 2, P])
        vg = sb("vg", [P, 4, 2 * P])
        ST = sb("ST", [P, 2, HEADS, P])
        go = sb("go", [P, P])
        xrow = sb("xrow", [P, XR, TOPK, ROW])
        th = sb("th", [P, 2, NE])
        sg = sb("sg", [P, NE])
        top = sb("top", [P, 8])
        topi = sb("topi", [P, 8], U32)
        idx = sb("idx", [P, 4, TOPK])
        OH = sb("OH", [P, 4, TOPK, NE], BF16)
        acc = sb("acc", [P, 3, NE], BF16)
        ssum = sb("ssum", [P, 1])
        srec = sb("srec", [P, 1])
        mpos = sb("mpos", [P, TOPK, NE])
        pos = sb("pos", [P, TOPK])
        over = sb("over", [P, TOPK])
        place = sb("place", [P, TOPK])
        slots = sb("slots", [P, TOPK, NT], U32)

        NW = 6
        NY = 4
        xb = sb("xb", [P, NW, EG, ROW])
        w13s = sb("w13s", [P, NW, EG, P])
        w2s = sb("w2s", [P, NW, EG, P])
        xbT = sb("xbT", [P, 2, EG, BLK])
        gs = sb("gs", [P, 2, EG * BLK])
        hT = sb("hT", [P, 2, EG, BLK])
        ys = sb("ys", [P, NY, EG, P])
        shg = sb("shg", [P, GN])
        shT = sb("shT", [P, TG, P])
        ovv = sb("ovv", [P, NE])
        ovw = sb("ovw", [P, NE])
        ovl = sb("ovl", [P, NOV])
        ovf = sb("ovf", [P, NOV])
        ovrow = sb("ovrow", [P, NOV], I32)
        ovexp = sb("ovexp", [P, NOV], I32)
        ovc = sb("ovc", [P, 8])
        ovs = sb("ovs", [P, 1])
        ovn = sb("ovn", [P, 1], I32)
        pr = X[:, :, :, :].rearrange("p a c n -> p (a c n)")[:, 0:NT * TOPK * P].rearrange(
            "p (t k d) -> p t k d", t=NT, k=TOPK)

        bank = [ctx.enter_context(nc.psum_tensor(f"bank{n}", [P, 512], F32)) for n in range(8)]
        CONV, A, TR, QK, VG, S0, S1, O = bank
        XT = bank[0:2]
        GU = bank[2:4]
        Y = bank[4:6]
        SH1, SH3 = bank[6:8]

        c_in, v_in, r_in, sq_in, we_in = sem("c_in"), sem("v_in"), sem("r_in"), sem("sq_in"), sem("we_in")
        wp_in = [sem("wp_in0"), sem("wp_in1")]
        x_in = [[sem(f"x_in{n}_{part}") for part in range(3)] for n in range(2)]
        filled_tile, filled, zeroed = sem("filled_tile"), sem("filled"), sem("zeroed")
        ones_set = sem("ones_set")
        w_ready, wd_in_ready, wd_ps, wd_ready, cvec_ready, bqm_ready, before_ready = (sem(n) for n in (
            "w_ready", "wd_in_ready", "wd_ps", "wd_ready", "cvec_ready", "bqm_ready", "before_ready"))
        conv_ps, yT_ready = sem("conv_ps"), sem("yT_ready")
        y_ps, ystat, r1_ready, h_ready, hstat, r2_ready = (sem(n) for n in (
            "y_ps", "ystat", "r1_ready", "h_ready", "hstat", "r2_ready"))
        xn_ready, xnT_ps, xnT_ready = sem("xn_ready"), sem("xnT_ps"), sem("xnT_ready")
        qk_ps, vg_ps, qk_ready, vg_ready, g_ready = (sem(n) for n in (
            "qk_ps", "vg_ps", "qk_ready", "vg_ready", "g_ready"))
        s_ps, st_ready, av_ps, av_read, h2stat, r3_ready, h2_ready = (sem(n) for n in (
            "s_ps", "st_ready", "av_ps", "av_read", "h2stat", "r3_ready", "h2_ready"))
        xf_ready, x2T_ps, x2T_ready, lg_ps, th_ready, oh_ready, meta_ready = (sem(n) for n in (
            "xf_ready", "x2T_ps", "x2T_ready", "lg_ps", "th_ready", "oh_ready", "meta_ready"))
        acc_ready, pos_ps, pos_read, slot_ready = (sem(n) for n in (
            "acc_ready", "pos_ps", "pos_read", "slot_ready"))
        sent = [sem(f"sent{n}") for n in range(XR)]
        dve_step, pool_step = sem("dve_step"), sem("pool_step")
        count_ps, list_ready = sem("count_ps"), sem("list_ready")
        xb_in = [sem(f"xb_in{n}") for n in range(NW)]
        ew_in = [sem(f"ew_in{n}") for n in range(NW)]
        xbT_ps, xbT_ready, gu_ps, gs_ready, hT_ready, ey_ps, ys_ready = (sem(n) for n in (
            "xbT_ps", "xbT_ready", "gu_ps", "gs_ready", "hT_ready", "ey_ps", "ys_ready"))
        put = [sem(f"put{n}") for n in range(NY)]
        sh_ps, shg_ready, shT_ready, so_ps, so_ready = (sem(n) for n in (
            "sh_ps", "shg_ready", "shT_ready", "so_ps", "so_ready"))
        pr_in = [sem(f"pr_in{n}") for n in range(NG)]
        fin_ready, stored = sem("fin_ready"), sem("stored")

        block = ctx.enter_context(nc.Block())

        NB = NEG + 1
        MORE = NOV // EG - 1
        LAST = NT + 5
        FILLS = (NE + 1) * CAP // P // FILLR
        FREST = (NE + 1) * CAP // P - FILLS * FILLR

        @block.sync
        def _(sp):
            HC = NCH // 2

            def load_group(g):
                if g >= 2:
                    sp.wait_ge(conv_ps, g - 1)
                for n in range(2):
                    if g == 0:
                        sp.dma_start(WP[:, n], wp[n]).then_inc(wp_in[n], 16)
                    sp.dma_start(X[:, g % 2, n * HC:(n + 1) * HC], xp[g, :, n * HC:(n + 1) * HC]
                                 ).then_inc(x_in[g % 2][n], 16)
                sp.dma_start(XE[:, g % 2], xe[g]).then_inc(x_in[g % 2][2], 16)

            load_group(0)
            sp.dma_start(WE[:, :, :], we.rearrange("(c k) d -> k c d", k=2 * EDGE)).then_inc(we_in, 16)
            sp.dma_start(V[:, :], vecs).then_inc(v_in, 16)
            sp.dma_start(SQ[:, :], sq).then_inc(sq_in, 16)
            sp.dma_start(C[:, :], cst).then_inc(c_in, 16)
            sp.dma_start(R[:, :], rows.partition_broadcast(P)).then_inc(r_in, 16)
            sp.dma_start(destv[:, :, :], dest.rearrange("p (t k) -> p t k", k=TOPK)).then_inc(r_in, 16)
            load_group(1)
            sp.wait_ge(filled_tile, 2)
            bufv = buf.rearrange("(p r) w -> p r w", p=P)
            for n in range(FILLS):
                if n == 3:
                    load_group(2)
                sp.dma_start(bufv[:, n * FILLR:(n + 1) * FILLR], fill[:, :, :]).then_inc(filled, 16)
            if FREST:
                sp.dma_start(bufv[:, FILLS * FILLR:], fill[:, 0:FREST]).then_inc(filled, 16)
            pairv = pair.rearrange("(p r) w -> p (r w)", p=P)
            for n in range(2):
                sp.dma_start(pairv[:, n * 2048:(n + 1) * 2048], zero[:, :]).then_inc(zeroed, 16)
            load_group(3)

            def load_weights(q):
                if q >= NW:
                    sp.wait_ge(ey_ps, q - NW + 1)
                sp.dma_start(w13s[:, q % NW], w13[q * EG:(q + 1) * EG].rearrange("e d n -> d e n")
                             ).then_inc(ew_in[q % NW], 16)
                sp.dma_start(w2s[HID:P, q % NW], w2[q * EG:(q + 1) * EG].rearrange("e d n -> d e n")
                             ).then_inc(ew_in[q % NW], 16)

            def load_rows(q):
                if q >= NW:
                    sp.wait_ge(ys_ready, q - NW + 1)
                    sp.wait_ge(put[(q - NW) % NY], 16 * EG * ((q - NW) // NY + 1))
                sp.dma_start(xb[:, q % NW],
                             buf[q * EG * CAP:(q + 1) * EG * CAP].rearrange("(e s) w -> s e w", e=EG)[0:BLK]
                             ).then_inc(xb_in[q % NW], 16)

            def load_overflow(n, parity):
                for e in range(EG):
                    row = sp.value_load(ovrow[0:1, bass.ds(n * EG + e, 1)], min_val=0, max_val=NE * CAP + BLK)
                    exp = sp.value_load(ovexp[0:1, bass.ds(n * EG + e, 1)], min_val=0, max_val=NE - 1)
                    sp.dma_start(xb[:, parity, e], buf[bass.ds(row, BLK), :]).then_inc(xb_in[parity], 16)
                    sp.dma_start(w13s[:, parity, e],
                                 w13[bass.ds(exp, 1)].rearrange("e d n -> (e d) n")).then_inc(ew_in[parity], 16)
                    sp.dma_start(w2s[HID:P, parity, e],
                                 w2[bass.ds(exp, 1)].rearrange("e d n -> (e d) n")).then_inc(ew_in[parity], 16)

            for q in range(NW):
                load_weights(q)
            for n in range(XR):
                sp.wait_ge(sent[n], 16 * TOPK * (NT // XR))
            for q in range(NW):
                load_rows(q)
            for q in range(NW, NEG):
                load_weights(q)
                load_rows(q)
            q = NEG
            sp.wait_ge(list_ready, 1)
            sp.wait_ge(ey_ps, q - NW + 1)
            sp.wait_ge(ys_ready, q - NW + 1)
            sp.wait_ge(put[(q - NW) % NY], 16 * EG * ((q - NW) // NY + 1))
            load_overflow(0, q % NW)
            more = sp.value_load(ovn[0:1, 0:1], min_val=0, max_val=NOV // EG - 1)
            for n in range(NY):
                sp.wait_ge(put[n], 16 * EG * len(range(n, NB, NY)))
            for n in range(MORE):
                with sp.If(more > n):
                    load_overflow(n + 1, 0)
                    sp.wait_ge(put[0], 16 * EG * (len(range(0, NB, NY)) + n + 1))
            pv = pair.rearrange("(t p k) w -> p t k w", p=P, k=TOPK)
            for g in range(NG):
                sp.dma_start(pr[:, g * TG:(g + 1) * TG], pv[:, g * TG:(g + 1) * TG]).then_inc(pr_in[g], 16)
            ov = out.rearrange("(t p) d -> p t d", p=P)
            for g in range(NG):
                sp.wait_ge(fin_ready, g + 1)
                sp.dma_start(ov[:, g * TG:(g + 1) * TG], h[:, g * TG:(g + 1) * TG]).then_inc(stored, 16)
            sp.wait_ge(stored, 16 * NG)

        @block.tensor
        def _(pe):
            HC = NCH // 2

            def conv(g, j):
                if j % HC == 0:
                    pe.wait_ge(x_in[g % 2][j // HC], 16 * (g // 2 + 1))
                    if g == 0 and j < NCH:
                        pe.wait_ge(w_ready, j // HC + 1)
                    if g == 0 and j == NCH:
                        pe.wait_ge(we_in, 16)
                if j == 0 and g >= 1:
                    pe.wait_ge(yT_ready, g)
                if j < NCH:
                    w, x = W[:, j], X[:, g % 2, j]
                else:
                    w, x = WE[:, j - NCH], XE[:, g % 2, j - NCH]
                mm = nc.tensor.matmul(CONV[:, :], w, x, start=(j == 0), stop=(j == NCH + 1))
                if j == NCH + 1:
                    mm.then_inc(conv_ps, 1)

            def embed(t):
                pe.wait_ge(yT_ready, t // TG + 1)
                if t >= 1:
                    pe.wait_ge(h_ready, t)
                y = yT[:, t // TG % 2, t % TG * P:(t % TG + 1) * P]
                nc.tensor.transpose(A[:, 0:P], y, ident)
                nc.tensor.matmul(A[:, P:2 * P], y, WD[:, :], start=True, stop=True).then_inc(y_ps, 1)

            def turn_xn(t):
                pe.wait_ge(xn_ready, t + 1)
                if t >= 4:
                    pe.wait_ge(x2T_ready, t - 3)
                nc.tensor.transpose(TR[:, 0:P], xn[:, t % 2], ident).then_inc(xnT_ps, 1)

            def project(t):
                pe.wait_ge(xnT_ready, t + 1)
                if t >= 1:
                    pe.wait_ge(qk_ready, t)
                nc.tensor.matmul(QK[:, 0:P], wq, xnT[:, t % 2], start=True, stop=True)
                nc.tensor.matmul(QK[:, P:2 * P], wk, xnT[:, t % 2], start=True, stop=True).then_inc(qk_ps, 1)
                if t >= 1:
                    pe.wait_ge(vg_ready, t)
                nc.tensor.matmul(VG[:, 0:2 * P], xnT[:, t % 2], wvg, start=True, stop=True).then_inc(vg_ps, 1)

            def scores(t):
                pe.wait_ge(qk_ready, t + 1)
                if t >= 1:
                    pe.wait_ge(st_ready, 2 * t)
                half = P // 2
                for n, s in enumerate((S0, S1)):
                    mm = nc.tensor.matmul(s[:, :], kT[n * half:(n + 1) * half, t % 2],
                                          qm[n * half:(n + 1) * half, t % 2].rearrange("p a i -> p (a i)"),
                                          start=True, stop=True)
                mm.then_inc(s_ps, 1)

            def attend(t, n):
                if n == 0:
                    pe.wait_ge(vg_ready, t + 1)
                    if t >= 2:
                        pe.wait_ge(th_ready, t - 1)
                pe.wait_ge(st_ready, 2 * t + n + 1)
                for hh in range(n * QM, (n + 1) * QM):
                    mm = nc.tensor.matmul(O[:, hh * HD:(hh + 1) * HD], ST[:, t % 2, hh],
                                          vg[:, t % 4, hh * HD:(hh + 1) * HD], start=True, stop=True)
                if n == 1:
                    mm.then_inc(av_ps, 1)

            def places(t):
                pe.wait_ge(oh_ready, t + 1)
                if t == 0:
                    pe.wait_ge(before_ready, 1)
                    pe.wait_ge(ones_set, 1)
                if t >= 1:
                    pe.wait_ge(acc_ready, t)
                pe.wait_ge(av_read, min(t + 3, NT))
                pe.wait_ge(th_ready, t + 1)
                for k in range(TOPK):
                    mm = nc.tensor.matmul(O[:, 0:NE], before[:, :], OH[:, t % 4, k],
                                          start=(k == 0), stop=(t == 0 and k == TOPK - 1))
                if t >= 1:
                    mm = nc.tensor.matmul(O[:, 0:NE], ones[:, :], acc[:, t % 3], start=False, stop=True)
                mm.then_inc(pos_ps, 1)

            def turn_xf(t):
                pe.wait_ge(xf_ready, t + 1)
                pe.wait_ge(xnT_ready, min(t + 4, NT))
                nc.tensor.transpose(TR[:, 0:P], xrow[:, t % XR, 0, 0:P], ident).then_inc(x2T_ps, 1)

            def logits(t):
                pe.wait_ge(x2T_ready, t + 1)
                if t >= 1:
                    pe.wait_ge(pos_read, t)
                pe.wait_ge(av_read, min(t + 2, NT))
                nc.tensor.matmul(O[:, 0:NE], x2T[:, t], gw, start=True, stop=True).then_inc(lg_ps, 1)

            for j in range(NCH + 2):
                conv(0, j)
            pe.wait_ge(c_in, 16)
            pe.wait_ge(sq_in, 16)
            pe.wait_ge(wd_in_ready, 1)
            nc.tensor.matmul(QK[:, 0:P], center, gdw[:, :], start=True, stop=True)
            nc.tensor.matmul(VG[:, 0:P], betab[:, :], dw, start=True, stop=True).then_inc(wd_ps, 1)
            pe.wait_ge(wd_ready, 1)
            pe.wait_ge(cvec_ready, 1)

            def conv_step(i, n):
                g, j = (i + 1) // TG + 1, 2 * ((i + 1) % TG) + n
                if i == 0:
                    conv(g, n)
                if g < NG:
                    conv(g, j)

            embed(0)
            for i in range(LAST):
                if 0 <= i - 2 < NT:
                    scores(i - 2)
                if 0 <= i - 4 < NT:
                    turn_xf(i - 4)
                if 0 <= i - 3 < NT:
                    attend(i - 3, 0)
                if 0 <= i - 1 < NT:
                    project(i - 1)
                if 0 <= i - 3 < NT:
                    attend(i - 3, 1)
                conv_step(i, 0)
                if i < NT:
                    turn_xn(i)
                if 0 <= i - 5 < NT:
                    places(i - 5)
                if i + 1 < NT:
                    embed(i + 1)
                conv_step(i, 1)
                if 0 <= i - 4 < NT:
                    logits(i - 4)
            pe.wait_ge(acc_ready, NT)
            pe.wait_ge(pos_read, NT)
            nc.tensor.matmul(O[:, 0:NE], ones[:, :], acc[:, NT % 3], start=True, stop=True).then_inc(count_ps, 1)

            def turn_rows(q, u, v=0, first=False, back=2):
                if not first:
                    pe.wait_ge(xbT_ready, q - back + 1)
                for e in range(EG):
                    mm = nc.tensor.transpose(XT[u][:, e * BLK:(e + 1) * BLK], xb[:, v, e, 0:P], ident)
                mm.then_inc(xbT_ps, 1)

            def gate_up(q, u, v=0, first=False, back=2):
                if not first:
                    pe.wait_ge(hT_ready, q - back + 1)
                pe.wait_ge(xbT_ready, q + 1)
                for e in range(EG):
                    mm = nc.tensor.matmul(GU[u][:, e * BLK:(e + 1) * BLK], w13s[:, v, e], xbT[:, u, e],
                                          start=True, stop=True)
                mm.then_inc(gu_ps, 1)

            def down(q, u, v=0, first=False, back=2):
                if not first:
                    pe.wait_ge(ys_ready, q - back + 1)
                pe.wait_ge(hT_ready, q + 1)
                for e in range(EG):
                    mm = nc.tensor.matmul(Y[u][:, e * P:(e + 1) * P], hT[HID:P, u, e], w2s[HID:P, v, e],
                                          start=True, stop=True)
                mm.then_inc(ey_ps, 1)

            def shared_up(g):
                if g == 0:
                    pe.wait_ge(x2T_ready, NT)
                    pe.wait_ge(st_ready, 2 * NT)
                    pe.wait_ge(list_ready, 1)
                else:
                    pe.wait_ge(so_ready, g)
                x = x2T[:, g * TG:(g + 1) * TG].rearrange("p t n -> p (t n)")
                nc.tensor.matmul(SH1[:, :], s1, x, start=True, stop=True)
                nc.tensor.matmul(SH3[:, :], s3, x, start=True, stop=True).then_inc(sh_ps, 1)

            def shared_down(g):
                pe.wait_ge(shT_ready, g + 1)
                for n in range(TG):
                    mm = nc.tensor.matmul(SH1[:, n * P:(n + 1) * P], shT[:, n], s2, start=True, stop=True)
                mm.then_inc(so_ps, 1)

            shared_up(0)
            shared_down(0)
            for i in range(NB + 2):
                if i < NB:
                    pe.wait_ge(xb_in[i % NW], 16 * (i // NW) + (16 if i < NEG else 16 * EG))
                    turn_rows(i, i % 2, i % NW, first=i < 2)
                if 0 <= i - 1 < NB:
                    q = i - 1
                    pe.wait_ge(ew_in[q % NW], 32 * (q // NW) + (32 if q < NEG else 32 * EG))
                    gate_up(q, q % 2, q % NW, first=q < 2)
                if 0 <= i - 2 < NB:
                    down(i - 2, (i - 2) % 2, (i - 2) % NW, first=i - 2 < 2)
                if i in (3, 6, 9):
                    shared_up(i // 3)
                if i in (4, 7, 10):
                    shared_down(i // 3)
            more = pe.value_load(ovn[0:1, 0:1], min_val=0, max_val=NOV // EG - 1)
            for n in range(MORE):
                with pe.If(more > n):
                    pe.wait_ge(xb_in[0], 16 * len(range(0, NEG, NW)) + (n + 1) * 16 * EG)
                    pe.wait_ge(ew_in[0], 32 * len(range(0, NEG, NW)) + (n + 1) * 32 * EG)
                    turn_rows(n + NB, 0, back=1)
                    gate_up(n + NB, 0, back=1)
                    down(n + NB, 0, back=1)

        @block.scalar
        def _(act):
            def evac_y(g):
                act.wait_ge(conv_ps, g + 1)
                if g == 0:
                    act.wait_ge(v_in, 16)
                if g >= 2:
                    act.wait_ge(y_ps, TG * (g - 1))
                nc.scalar.activation(yT[:, g % 2].rearrange("d (b p) -> d b p", p=T),
                                     CONV[:, :].rearrange("d (p b) -> d b p", p=T),
                                     ACT.Identity, bias=conv_b).then_inc(yT_ready, 1)

            def evac_xn(t):
                act.wait_ge(xnT_ps, t + 1)
                if t >= 2:
                    act.wait_ge(vg_ps, t - 1)
                nc.scalar.activation(xnT[:, t % 2], TR[:, 0:P], ACT.Copy).then_inc(xnT_ready, 1)

            def evac_qk(t):
                act.wait_ge(qk_ps, t + 1)
                if t == 0:
                    act.wait_ge(bqm_ready, 1)
                if t >= 2:
                    act.wait_ge(s_ps, t - 1)
                for m in range(QM):
                    nc.scalar.activation(qm[:, t % 2, m], QK[:, 0:P], ACT.Identity,
                                         bias=bqm[:, m:m + 1], scale=head[:, m:m + 1])
                nc.scalar.activation(kT[:, t % 2], QK[:, P:2 * P], ACT.Identity, bias=bk).then_inc(qk_ready, 1)

            def gates(t):
                act.wait_ge(vg_ready, t + 1)
                nc.scalar.activation(vg[:, t % 4, P:2 * P], vg[:, t % 4, P:2 * P], ACT.Silu).then_inc(g_ready, 1)

            def evac_xf(t):
                act.wait_ge(x2T_ps, t + 1)
                nc.scalar.activation(x2T[:, t], TR[:, 0:P], ACT.Copy).then_inc(x2T_ready, 1)

            def tanhs(t):
                act.wait_ge(lg_ps, t + 1)
                if t >= 2:
                    act.wait_ge(oh_ready, t - 1)
                nc.scalar.activation(th[:, t % 2], O[:, 0:NE], ACT.Tanh, scale=0.5).then_inc(th_ready, 1)

            evac_y(0)
            act.wait_ge(wd_ps, 1)
            nc.scalar.activation(WD[:, :], QK[:, 0:P], ACT.Copy).then_inc(wd_ready, 1)
            for i in range(LAST):
                if 0 <= i - 4 < NT:
                    evac_xf(i - 4)
                if 0 <= i - 1 < NT:
                    evac_qk(i - 1)
                    gates(i - 1)
                if i < NT:
                    evac_xn(i)
                if i % TG == 2 and i // TG + 1 < NG:
                    evac_y(i // TG + 1)
                if 0 <= i - 4 < NT:
                    tanhs(i - 4)

            def evac_rows(q, u, v=0, first=False, back=2):
                act.wait_ge(xbT_ps, q + 1)
                if not first:
                    act.wait_ge(gu_ps, q - back + 1)
                nc.scalar.activation(xbT[:, u].rearrange("p e s -> p (e s)"), XT[u][:, :], ACT.Copy
                                     ).then_inc(xbT_ready, 1)

            def gate(q, u, v=0, first=False, back=2):
                act.wait_ge(gu_ps, q + 1)
                if not first:
                    act.wait_ge(hT_ready, q - back + 1)
                nc.scalar.activation(gs[HID:P, u], GU[u][0:HID, :], ACT.Silu).then_inc(gs_ready, 1)

            def shared_gate(g):
                act.wait_ge(sh_ps, g + 1)
                if g >= 1:
                    act.wait_ge(shT_ready, g)
                nc.scalar.activation(shg[:, :], SH1[:, :], ACT.Silu).then_inc(shg_ready, 1)

            shared_gate(0)
            for i in range(NB + 1):
                if i < NB:
                    evac_rows(i, i % 2, first=i < 2)
                if 0 <= i - 1 < NB:
                    gate(i - 1, (i - 1) % 2, first=i - 1 < 2)
                if i in (3, 6, 9):
                    shared_gate(i // 3)
            more = act.value_load(ovn[0:1, 0:1], min_val=0, max_val=NOV // EG - 1)
            for n in range(MORE):
                with act.If(more > n):
                    evac_rows(n + NB, 0, back=1)
                    gate(n + NB, 0, back=1)

        @block.vector
        def _(dve):
            steps = [0]

            def own(ins):
                steps[0] += 1
                ins.then_inc(dve_step, 1)
                dve.wait_ge(dve_step, steps[0])

            HC = NCH // 2
            for n in range(2):
                dve.wait_ge(wp_in[n], 16)
                c = slice(n * HC, (n + 1) * HC)
                own(nc.vector.tensor_tensor(W[:, c], WP[:, n, 0], WP[:, n, 1], ALU.add))
                for s in range(2, 5):
                    ins = nc.vector.tensor_tensor(W[:, c], W[:, c], WP[:, n, s], ALU.add)
                    if s == 4:
                        ins.then_inc(w_ready, 1)
                    else:
                        own(ins)
            dve.wait_ge(v_in, 16)
            dve.wait_ge(sq_in, 16)
            nc.vector.tensor_scalar(gdw[:, :], dw, gamma, None, ALU.mult)
            nc.vector.tensor_copy(betab[:, :], beta.to_broadcast([P, P])).then_inc(wd_in_ready, 1)
            dve.wait_ge(c_in, 16)
            nc.vector.tensor_copy(before[:, :], before_f).then_inc(before_ready, 1)
            nc.vector.tensor_scalar(bqm[:, :], head, bq, None, ALU.mult).then_inc(bqm_ready, 1)
            dve.wait_ge(r_in, 32)
            dve.wait_ge(wd_ps, 1)
            nc.vector.tensor_tensor(cvec[:, :], VG[:, 0:P], dense_bias, ALU.add).then_inc(cvec_ready, 1)

            def step(ins):
                steps[0] += 1
                ins.then_inc(dve_step, 1)
                return steps[0]

            def head_steps(i):
                y, c = i < NT, 0 <= i - 5 < NT
                t, u = i, i - 5
                if y:
                    dve.wait_ge(y_ps, t + 1)
                    y1 = step(nc.vector.bn_stats(st1[:, t % 2], A[:, 0:P]))
                if c:
                    dve.wait_ge(th_ready, u + 1)
                    c1 = step(nc.vector.tensor_scalar(sg[:, :], th[:, u % 2], 0.5, 0.5, ALU.mult, ALU.add))
                if y:
                    dve.wait_ge(dve_step, y1)
                    nc.vector.bn_aggr(mv1[:, t % 2], st1[:, t % 2]).then_inc(ystat, 1)
                if c:
                    dve.wait_ge(dve_step, c1)
                    c2 = step(nc.vector.max(top[:, :], sg[:, :]))
                    dve.wait_ge(dve_step, c2)
                    c3 = step(nc.vector.max_index(topi[:, :], top[:, :], sg[:, :]))
                    c6 = step(nc.vector.tensor_scalar(ssum[:, :], top[:, 0:1], top[:, 1:2], 1e-20,
                                                      ALU.add, ALU.add))
                    dve.wait_ge(dve_step, c3)
                    c4 = step(nc.vector.tensor_copy(idx[:, u % 4], topi[:, 0:TOPK]))
                    dve.wait_ge(dve_step, c6)
                    c7 = step(nc.vector.reciprocal(srec[:, :], ssum[:, :]))
                    if u >= 4:
                        dve.wait_ge(pos_ps, u - 3)
                        dve.wait_ge(acc_ready, u - 3)
                    dve.wait_ge(dve_step, c4)
                    nc.vector.tensor_tensor(OH[:, u % 4], expert.unsqueeze(1).broadcast_to([P, TOPK, NE]),
                                            idx[:, u % 4].unsqueeze(2).broadcast_to([P, TOPK, NE]),
                                            ALU.is_equal).then_inc(oh_ready, 1)
                    dve.wait_ge(dve_step, c7)
                    if u >= XR:
                        dve.wait_ge(sent[u % XR], 16 * TOPK * (u // XR))
                    nc.vector.tensor_scalar(xrow[:, u % XR, :, P], top[:, 0:TOPK], srec[:, 0:1], ROUTE_SCALE,
                                            ALU.mult, ALU.mult)
                if y:
                    dve.wait_ge(r1_ready, t + 1)
                    if t == 0:
                        dve.wait_ge(cvec_ready, 1)
                    nc.vector.scalar_tensor_tensor(out=h[:, t], in0=A[:, P:2 * P], scalar=rs1[:, t % 2],
                                                   in1=cvec[:, :], op0=ALU.mult, op1=ALU.add).then_inc(h_ready, 1)
                if y:
                    dve.wait_ge(h_ready, t + 1)
                    h2 = step(nc.vector.bn_stats(st2[:, t % 2], h[:, t]))
                if c:
                    nc.vector.tensor_copy(xrow[:, u % XR, :, P + 1].bitcast(I32), destv[:, u]).then_inc(meta_ready, 1)
                if y:
                    dve.wait_ge(dve_step, h2)
                    nc.vector.bn_aggr(mv2[:, t % 2], st2[:, t % 2]).then_inc(hstat, 1)

            def middle_steps(i):
                a, f = 0 <= i - 3 < NT, 0 <= i - 5 < NT
                t, u = i - 3, i - 5
                if a:
                    dve.wait_ge(av_ps, t + 1)
                    dve.wait_ge(g_ready, t + 1)
                    nc.vector.tensor_tensor(go[:, :], O[:, 0:P], vg[:, t % 4, P:2 * P], ALU.mult
                                            ).then_inc(av_read, 1)
                if a:
                    dve.wait_ge(av_read, t + 1)
                    nc.vector.tensor_tensor(h[:, t], h[:, t], go[:, :], ALU.add).then_inc(h2_ready, 1)
                if f:
                    dve.wait_ge(pos_ps, u + 1)
                    nc.vector.tensor_tensor(mpos[:, :, :], O[:, 0:NE].unsqueeze(1).broadcast_to([P, TOPK, NE]),
                                            OH[:, u % 4], ALU.mult).then_inc(pos_read, 1)
                if f:
                    dve.wait_ge(pos_read, u + 1)
                    f2 = step(nc.vector.tensor_reduce(pos[:, :], mpos[:, :, :], AX.X, ALU.add))
                if a:
                    dve.wait_ge(h2_ready, t + 1)
                    a3 = step(nc.vector.bn_stats(st3[:, t % 2], h[:, t]))
                if f:
                    dve.wait_ge(dve_step, f2)
                    step(nc.vector.tensor_scalar(over[:, :], pos[:, :], CAP - 0.5, float(BIG),
                                                 ALU.is_gt, ALU.mult))
                    f4 = step(nc.vector.scalar_tensor_tensor(out=place[:, :], in0=idx[:, u % 4],
                                                             scalar=float(CAP), in1=pos[:, :],
                                                             op0=ALU.mult, op1=ALU.add))
                if a:
                    dve.wait_ge(dve_step, a3)
                    nc.vector.bn_aggr(mv3[:, t % 2], st3[:, t % 2]).then_inc(h2stat, 1)
                if f:
                    dve.wait_ge(dve_step, f4)
                    nc.vector.tensor_tensor(slots[:, :, u], over[:, :], place[:, :], ALU.add).then_inc(slot_ready, 1)

            def bias_vg(t):
                dve.wait_ge(vg_ps, t + 1)
                if t >= 4:
                    dve.wait_ge(av_ps, t - 3)
                nc.vector.tensor_tensor(vg[:, t % 4], VG[:, 0:2 * P], vg_bias, ALU.add).then_inc(vg_ready, 1)

            def norm_h(t):
                dve.wait_ge(r2_ready, t + 1)
                if t >= 2:
                    dve.wait_ge(xnT_ps, t - 1)
                nc.vector.tensor_scalar(xn[:, t % 2], h[:, t], mv2[:, t % 2, 0:1], rs2[:, t % 2],
                                        ALU.subtract, ALU.mult).then_inc(xn_ready, 1)

            def norm_h2(t):
                dve.wait_ge(r3_ready, t + 1)
                if t >= XR:
                    dve.wait_ge(sent[t % XR], 16 * TOPK * (t // XR))
                    dve.wait_ge(x2T_ps, t - XR + 1)
                nc.vector.tensor_scalar(xrow[:, t % XR, :, 0:P], h[:, t:t + 1].broadcast_to([P, TOPK, P]),
                                        mv3[:, t % 2, 0:1], rs3[:, t % 2],
                                        ALU.subtract, ALU.mult).then_inc(xf_ready, 1)

            def decay_scores(t):
                dve.wait_ge(s_ps, t + 1)
                if t >= 2:
                    dve.wait_ge(av_ps, t - 1)
                for n, s in enumerate((S0, S1)):
                    nc.vector.tensor_tensor(
                        ST[:, t % 2, n * QM:(n + 1) * QM].rearrange("p a i -> p (a i)"), s[:, :],
                        decay[:, n * 512:(n + 1) * 512], ALU.mult).then_inc(st_ready, 1)

            for i in range(LAST):
                head_steps(i)
                if 0 <= i - 2 < NT:
                    decay_scores(i - 2)
                if i < NT:
                    norm_h(i)
                if 0 <= i - 1 < NT:
                    bias_vg(i - 1)
                middle_steps(i)
                if 0 <= i - 3 < NT:
                    norm_h2(i - 3)

            dve.wait_ge(count_ps, 1)
            own(nc.vector.scalar_tensor_tensor(out=ovv[:, :], in0=O[:, 0:NE], scalar=BLK + 0.5, in1=left,
                                               op0=ALU.is_gt, op1=ALU.mult))
            for n in range(NOV // 8):
                src, dst = (ovv, ovw) if n % 2 == 0 else (ovw, ovv)
                own(nc.vector.max(ovl[:, 8 * n:8 * n + 8], src[:, :]))
                if n < NOV // 8 - 1:
                    own(nc.vector.match_replace(dst[:, :], ovl[:, 8 * n:8 * n + 8], src[:, :], 0.0))
            own(nc.vector.tensor_scalar(ovf[:, :], ovl[:, :], -1.0, float(NE), ALU.mult, ALU.add))
            nc.vector.tensor_scalar(ovrow[:, :], ovf[:, :], float(CAP), float(BLK), ALU.mult, ALU.add)
            nc.vector.tensor_scalar(ovexp[:, :], ovf[:, :], float(NE - 1), None, ALU.min)
            own(nc.vector.tensor_scalar(ovc[:, :], ovl[:, ::EG], 0.5, None, ALU.is_gt))
            own(nc.vector.tensor_reduce(ovs[:, :], ovc[:, 1:], AX.X, ALU.add))
            nc.vector.tensor_copy(ovn[:, :], ovs[:, :]).then_inc(list_ready, 1)

            def hidden(q, u, v=0, first=False, back=2):
                dve.wait_ge(gs_ready, q + 1)
                if not first:
                    dve.wait_ge(ey_ps, q - back + 1)
                nc.vector.tensor_tensor(hT[HID:P, u].rearrange("p e s -> p (e s)"), GU[u][HID:P, :],
                                        gs[HID:P, u], ALU.mult).then_inc(hT_ready, 1)

            def weigh(q, u, v=0, first=False, back=2):
                dve.wait_ge(ey_ps, q + 1)
                z = q % NY if q < NB else 0
                if q >= NY:
                    dve.wait_ge(put[z], 16 * EG * (q // NY if q < NB else q - NB + len(range(0, NB, NY))))
                nc.vector.tensor_tensor(ys[:, z], Y[u][:, :].rearrange("p (e n) -> p e n", e=EG),
                                        xb[:, v, :, P:P + 1].broadcast_to([P, EG, P]),
                                        ALU.mult).then_inc(ys_ready, 1)

            def shared_hidden(g):
                dve.wait_ge(shg_ready, g + 1)
                if g >= 1:
                    dve.wait_ge(so_ps, g)
                nc.vector.tensor_tensor(shT[:, :].rearrange("p t n -> p (t n)"), SH3[:, :], shg[:, :],
                                        ALU.mult).then_inc(shT_ready, 1)

            def shared_add(g):
                dve.wait_ge(so_ps, g + 1)
                hg = h[:, g * TG:(g + 1) * TG].rearrange("p t n -> p (t n)")
                nc.vector.tensor_tensor(hg, SH1[:, :], hg, ALU.add).then_inc(so_ready, 1)

            shared_hidden(0)
            shared_add(0)
            for i in range(NB + 2):
                if 0 <= i - 1 < NB:
                    hidden(i - 1, (i - 1) % 2, first=i - 1 < 2)
                if 0 <= i - 2 < NB:
                    weigh(i - 2, (i - 2) % 2, (i - 2) % NW, first=i - 2 < 2)
                if i in (3, 6, 9):
                    shared_hidden(i // 3)
                if i in (4, 7, 10):
                    shared_add(i // 3)
            more = dve.value_load(ovn[0:1, 0:1], min_val=0, max_val=NOV // EG - 1)
            for n in range(MORE):
                with dve.If(more > n):
                    hidden(n + NB, 0, back=1)
                    weigh(n + NB, 0, back=1)

            for g in range(NG):
                dve.wait_ge(pr_in[g], 16)
                dve.wait_ge(so_ready, g + 1)
                t = slice(g * TG, (g + 1) * TG)
                own(nc.vector.tensor_tensor(h[:, t], h[:, t], pr[:, t, 0], ALU.add))
                nc.vector.tensor_tensor(h[:, t], h[:, t], pr[:, t, 1], ALU.add).then_inc(fin_ready, 1)

        @block.gpsimd
        def _(pool):
            steps = [0]

            def own(ins):
                steps[0] += 1
                ins.then_inc(pool_step, 1)
                pool.wait_ge(pool_step, steps[0])

            own(pool.memset(fill[:, :, :], 0.0))
            pool.memset(fill[:, :, P + 1:P + 2].bitcast(I32), BIG).then_inc(filled_tile, 1)
            pool.memset(zero[:, :], 0.0).then_inc(filled_tile, 1)
            pool.memset(mhalf[:, :], -0.5)
            pool.memset(acc[:, 0], 0.0)
            own(pool.memset(ones[:, :], 1.0))
            pool.sem_inc(ones_set, 1)

            def rstd(t, stat, eps, mv, ve, rs, ready):
                pool.wait_ge(stat, t + 1)
                own(pool.tensor_scalar(ve[:, t % 2], mv[:, t % 2, 1:2], 1.0, eps, ALU.mult, ALU.add))
                pool.tensor_tensor(rs[:, t % 2], ve[:, t % 2], mhalf[:, :], ALU.pow).then_inc(ready, 1)

            def accumulate(t):
                pool.wait_ge(oh_ready, t + 1)
                if t >= 2:
                    pool.wait_ge(pos_ps, t - 1)
                own(pool.tensor_tensor(acc[:, (t + 1) % 3], acc[:, t % 3], OH[:, t % 4, 0], ALU.add))
                pool.tensor_tensor(acc[:, (t + 1) % 3], acc[:, (t + 1) % 3], OH[:, t % 4, 1], ALU.add
                                   ).then_inc(acc_ready, 1)
                pool.wait_ge(acc_ready, t + 1)

            def send(t, k):
                pool.wait_ge(slot_ready, t + 1)
                pool.wait_ge(meta_ready, t + 1)
                if t == 0:
                    pool.wait_ge(filled, 16 * (FILLS + (FREST > 0)))
                pool.indirect_dma_start(
                    buf, bass.IndirectOffsetOnAxis(ap=slots[:, k, t:t + 1], axis=0),
                    xrow[:, t % XR, k], None, bounds_check=NE * CAP - 1, oob_is_err=False
                ).then_inc(sent[t % XR], 16)

            for i in range(LAST):
                if i < NT:
                    rstd(i, ystat, LN_TOK, mv1, ve1, rs1, r1_ready)
                if 0 <= i - 6 < NT:
                    send(i - 6, 0)
                if 0 <= i - 5 < NT:
                    accumulate(i - 5)
                if i < NT:
                    rstd(i, hstat, LN, mv2, ve2, rs2, r2_ready)
                if 0 <= i - 6 < NT:
                    send(i - 6, 1)
                if 0 <= i - 3 < NT:
                    rstd(i - 3, h2stat, LN, mv3, ve3, rs3, r3_ready)
            for k in range(TOPK):
                send(NT - 1, k)

            def scatter(q, z, v):
                pool.wait_ge(ys_ready, q + 1)
                for e in range(EG):
                    pool.indirect_dma_start(
                        pair, bass.IndirectOffsetOnAxis(ap=xb[:, v, e, P + 1:P + 2].bitcast(U32), axis=0),
                        ys[:, z, e], None, bounds_check=TOKENS * TOPK - 1, oob_is_err=False
                    ).then_inc(put[z], 16)

            pool.wait_ge(zeroed, 32)
            for q in range(NB):
                scatter(q, q % NY, q % NW)
            more = pool.value_load(ovn[0:1, 0:1], min_val=0, max_val=NOV // EG - 1)
            for n in range(MORE):
                with pool.If(more > n):
                    scatter(n + NB, 0, 0)


def kernel(x, L0_tok_conv_w, L0_tok_conv_b, L0_tok_gamma, L0_tok_beta, L0_tok_dense_w, L0_tok_dense_b,
           L0_attn_wq, L0_attn_bq, L0_attn_wk, L0_attn_bk, L0_attn_wv, L0_attn_bv, L0_attn_wg, L0_attn_bg,
           L0_ffn_gate_w, L0_ffn_w1, L0_ffn_w3, L0_ffn_w2, L0_ffn_sw1, L0_ffn_sw3, L0_ffn_sw2):
    import concourse.bacc as bacc
    from concourse.bass_utils import run_bass_kernel_spmd

    x = np.asarray(x)
    img = x.reshape(NG, GB, GRID, PATCH, GRID, PATCH, CH).transpose(0, 3, 5, 6, 2, 4, 1)
    xp = np.ascontiguousarray(img).reshape(NG, NCH, P, GN).transpose(0, 2, 1, 3)
    xe = np.zeros((NG, 4, EDGE, GRID, GRID, GB), x.dtype)
    xe[:, 0, :, 1:] = img[:, PATCH - 1].reshape(NG, EDGE, GRID, GRID, GB)[:, :, :-1]
    xe[:, 1, :, :-1] = img[:, 0].reshape(NG, EDGE, GRID, GRID, GB)[:, :, 1:]
    xe[:, 2, :, :, 1:] = img[:, :, PATCH - 1].reshape(NG, EDGE, GRID, GRID, GB)[:, :, :, :-1]
    xe[:, 3, :, :, :-1] = img[:, :, 0].reshape(NG, EDGE, GRID, GRID, GB)[:, :, :, 1:]
    xe = xe.reshape(NG, 2, 2 * EDGE, GN).transpose(0, 2, 1, 3)

    cw = np.asarray(L0_tok_conv_w).reshape(PATCH, PATCH, 5, CH, P)
    wp = np.zeros((5, PATCH, PATCH, CH, P), cw.dtype)
    wp[0] = cw[:, :, 0]
    wp[1, :, :-1] = cw[:, 1:, 1]
    wp[2, :, 1:] = cw[:, :-1, 2]
    wp[3, :-1] = cw[1:, :, 3]
    wp[4, 1:] = cw[:-1, :, 4]
    wp = wp.reshape(5, 2, NCH // 2, P, P).transpose(1, 3, 0, 2, 4)
    we = np.concatenate([cw[0, :, 3].reshape(EDGE, P), cw[PATCH - 1, :, 4].reshape(EDGE, P),
                         cw[:, 0, 1].reshape(EDGE, P), cw[:, PATCH - 1, 2].reshape(EDGE, P)])

    sq = np.concatenate([np.asarray(L0_tok_dense_w), np.asarray(L0_attn_wq).T, np.asarray(L0_attn_wk).T,
                         np.asarray(L0_attn_wv).T, np.asarray(L0_attn_wg).T, np.asarray(L0_ffn_sw1),
                         np.asarray(L0_ffn_sw3), np.asarray(L0_ffn_sw2), np.asarray(L0_ffn_gate_w).T], 1)
    w13 = np.concatenate([np.asarray(L0_ffn_w1), np.asarray(L0_ffn_w3)], 2)
    vecs = np.stack([np.asarray(v) for v in (L0_tok_conv_b, L0_tok_gamma, L0_tok_beta, L0_attn_bq, L0_attn_bk)], 1)
    rows = np.concatenate([np.asarray(L0_attn_bv), np.asarray(L0_attn_bg), np.asarray(L0_tok_dense_b)])
    cst, dest = constants()

    nc = bacc.Bacc("TRN2", target_bir_lowering=False, num_devices=1)
    arrays, args = {}, []
    for name, a in (("xp", xp), ("xe", xe), ("wp", wp), ("we", we), ("sq", sq), ("w13", w13),
                    ("w2", np.asarray(L0_ffn_w2)), ("vecs", vecs), ("rows", rows), ("cst", cst), ("dest", dest)):
        a = np.ascontiguousarray(a)
        arrays[name] = a
        args.append(nc.dram_tensor(name, a.shape, mybir.dt.from_np(a.dtype), kind="ExternalInput").ap())
    res = nc.dram_tensor("out", (TOKENS, P), F32, kind="ExternalOutput").ap()
    tower(nc, *args, res)
    r = run_bass_kernel_spmd(nc, [arrays], core_ids=[0])
    return np.asarray(r.results[0]["out"]).reshape(IMAGES, T, P)
```

```python
from contextlib import ExitStack

import numpy as np

import concourse.bass as bass
from concourse import mybir

F32 = mybir.dt.float32
BF16 = mybir.dt.bfloat16
I32 = mybir.dt.int32
U32 = mybir.dt.uint32
ALU = mybir.AluOpType
ACT = mybir.ActivationFunctionType
AX = mybir.AxisListType

P = 128
IMAGES, SIDE, CH = 128, 64, 3
PATCH = 16
GRID = SIDE // PATCH
T = GRID * GRID
TOKENS = IMAGES * T
NT = TOKENS // P
TG = 4
NG = NT // TG
GN = TG * P
TS = 2
NS = NT // TS
LATE = 6
GB = IMAGES // NG
KP = PATCH * PATCH * CH
NCH = KP // P
NL = 3
HC = NCH // NL
EDGE = PATCH * CH
HEADS = 8
HD = P // HEADS
QM = 4
NE = 64
TOPK = 2
CAP = 256
HID = 64
BLK = 128
EG = 4
NEG = NE // EG
NOV = 32
BIG = 1 << 20
LN_TOK, LN = 1e-3, 1e-5
ROUTE_SCALE = 2.5
ROWS = NE * CAP + NOV * BLK
assert (TOKENS * TOPK) // (BLK + 1) < NOV


def constants():
    ident = np.eye(P, dtype=np.float32)
    center = ident - np.float32(1.0 / P)
    gam = (1.0 - 2.0 ** (-5.0 - np.arange(HEADS, dtype=np.float32))).astype(np.float32)
    j, i = np.arange(P)[:, None], np.arange(P)[None, :]
    keep = (j // T == i // T) & (j >= i)
    decay = np.zeros((P, HEADS, P), np.float32)
    for h in range(HEADS):
        decay[:, h] = np.where(keep, gam[h] ** np.maximum(j - i, 0).astype(np.float32), 0.0)
    decay *= np.float32(HD ** -0.5)
    before = (j < i).astype(np.float32)
    expert = np.broadcast_to(np.arange(NE, dtype=np.float32), (P, NE))
    left = np.broadcast_to(NE - np.arange(NE, dtype=np.float32), (P, NE))
    head = (np.arange(P)[:, None] // HD % QM == np.arange(QM)[None, :]).astype(np.float32)
    flat = np.concatenate([ident, center, before, expert, left, head, decay.reshape(P, -1)], 1)
    return np.ascontiguousarray(flat, np.float32)


NC_CONST = 3 * P + 2 * NE + QM + HEADS * P


def tower(nc, xp, xe, wp, we, sq, w13, w2, vecs, rows, cst, out):
    ctx = ExitStack()
    with ctx:
        def sb(name, shape, dt=F32):
            return ctx.enter_context(nc.sbuf_tensor(name, shape, dt))

        def sem(name):
            return ctx.enter_context(nc.semaphore(name))

        buf = nc.dram_tensor("expert_rows", (ROWS, P), F32, kind="Internal").ap()

        C = sb("C", [P, NC_CONST])
        ident = C[:, 0:P]
        center = C[:, P:2 * P]
        before_f = C[:, 2 * P:3 * P]
        expert = C[:, 3 * P:3 * P + NE]
        left = C[:, 3 * P + NE:3 * P + 2 * NE]
        head = C[:, 3 * P + 2 * NE:3 * P + 2 * NE + QM]
        decay = C[:, 3 * P + 2 * NE + QM:NC_CONST]
        V = sb("V", [P, 5])
        conv_b, gamma, beta, bq, bk = (V[:, n:n + 1] for n in range(5))
        R = sb("R", [P, 3 * P])
        vg_bias, dense_bias = R[:, 0:2 * P], R[:, 2 * P:3 * P]
        SQ = sb("SQ", [P, 8 * P + NE])
        dw, wq, wk, wvg, s1, s3, s2, gw = (SQ[:, a:b] for a, b in (
            (0, P), (P, 2 * P), (2 * P, 3 * P), (3 * P, 5 * P), (5 * P, 6 * P), (6 * P, 7 * P),
            (7 * P, 8 * P), (8 * P, 8 * P + NE)))
        WP = sb("WP", [P, NL, 5, HC, P])
        W = sb("W", [P, NCH, P])
        WE = sb("WE", [2 * EDGE, 2, P])
        gdw = sb("gdw", [P, P])
        WD = sb("WD", [P, P])
        betab = sb("betab", [P, P])
        cvec = sb("cvec", [P, P])
        bqm = sb("bqm", [P, QM])
        before = sb("before", [P, P], BF16)
        ones = sb("ones", [P, P], BF16)
        mhalf = sb("mhalf", [P, 1])
        FILLR = 16
        fill = sb("fill", [P, FILLR, P])

        XR = 8
        X = sb("X", [P, 2, NCH, GN])
        XE = sb("XE", [2 * EDGE, 2, 2, GN])
        yT = sb("yT", [P, 2, GN])
        h = sb("h", [P, NT, P])
        x2T = sb("x2T", [P, NT, P])
        st1, st2, st3 = (sb(f"st{n}", [P, 2, 6]) for n in (1, 2, 3))
        mv1, mv2, mv3 = (sb(f"mv{n}", [P, 2, 2]) for n in (1, 2, 3))
        ve1, ve2, ve3 = (sb(f"ve{n}", [P, 2, 1]) for n in (1, 2, 3))
        rs1, rs2, rs3 = (sb(f"rs{n}", [P, 2, 1]) for n in (1, 2, 3))
        xn = sb("xn", [P, 2, P])
        xnT = sb("xnT", [P, 2, P])
        qm = sb("qm", [P, 2, QM, P])
        kT = sb("kT", [P, 2, 2, P])
        vg = sb("vg", [P, 4, 2 * P])
        ST = sb("ST", [P, 2, HEADS, P])
        go = sb("go", [P, P])
        xrow = sb("xrow", [P, XR, P])
        pw = sb("pw", [P, NT, TOPK])
        th = sb("th", [P, 2, NE])
        sg = sb("sg", [P, NE])
        top = sb("top", [P, 8])
        topi = sb("topi", [P, 8], U32)
        idx = sb("idx", [P, 4, TOPK])
        OH = sb("OH", [P, 4, TOPK, NE], BF16)
        acc = sb("acc", [P, 3, NE], BF16)
        ssum = sb("ssum", [P, 1])
        srec = sb("srec", [P, 1])
        mpos = sb("mpos", [P, TOPK, NE])
        pos = sb("pos", [P, TOPK])
        over = sb("over", [P, TOPK])
        place = sb("place", [P, TOPK])
        slots = sb("slots", [P, TOPK, NT], U32)

        NW = 6
        NY = 4
        xb = sb("xb", [P, NW + 1, EG, P])
        w13s = sb("w13s", [P, NW + 1, EG, P])
        w2s = sb("w2s", [P, NW + 1, EG, P])
        xbT = sb("xbT", [P, 2, EG, BLK])
        gs = sb("gs", [P, 2, EG * BLK])
        hT = sb("hT", [P, 2, EG, BLK])
        ys = sb("ys", [P, NY, EG, P])
        shg = sb("shg", [P, TS * P])
        shT = sb("shT", [P, TS, P])
        ovv = sb("ovv", [P, NE])
        ovw = sb("ovw", [P, NE])
        ovl = sb("ovl", [P, NOV])
        ovf = sb("ovf", [P, NOV])
        ovrow = sb("ovrow", [P, NOV], I32)
        ovexp = sb("ovexp", [P, NOV], I32)
        ovm = sb("ovm", [P, NOV])
        ova = sb("ova", [P, NOV])
        ovc = sb("ovc", [P, 8])
        ovs = sb("ovs", [P, 1])
        ovn = sb("ovn", [P, 1], I32)
        pr = X[:, :, :, :].rearrange("p a c n -> p (a c n)")[:, 0:NT * TOPK * P].rearrange(
            "p (t k d) -> p t k d", t=NT, k=TOPK)

        bank = [ctx.enter_context(nc.psum_tensor(f"bank{n}", [P, 512], F32)) for n in range(8)]
        CONV, A, TR, QK, VG, S0, S1, O = bank
        XT = A, S1
        GU = bank[2:4]
        Y = bank[4:6]
        SH1, SH3 = CONV[:, 0:TS * P], CONV[:, TS * P:2 * TS * P]

        c_in, decay_in, v_in, r_in, sq_in, we_in = (sem(n) for n in (
            "c_in", "decay_in", "v_in", "r_in", "sq_in", "we_in"))
        wp_in = [sem(f"wp_in{n}") for n in range(NL)]
        x_in = [[sem(f"x_in{n}_{part}") for part in range(NL + 1)] for n in range(2)]
        filled_tile, filled, pr_zeroed = sem("filled_tile"), sem("filled"), sem("pr_zeroed")
        spare_filled = sem("spare_filled")
        ones_set, kT_zeroed = sem("ones_set"), sem("kT_zeroed")
        w_ready, wd_in_ready, wd_ps, wd_ready, cvec_ready, bqm_ready, before_ready = (sem(n) for n in (
            "w_ready", "wd_in_ready", "wd_ps", "wd_ready", "cvec_ready", "bqm_ready", "before_ready"))
        conv_ps, yT_ready = sem("conv_ps"), sem("yT_ready")
        y_ps, ystat, r1_ready, h_ready, hstat, r2_ready = (sem(n) for n in (
            "y_ps", "ystat", "r1_ready", "h_ready", "hstat", "r2_ready"))
        xn_ready, xnT_ps, xnT_ready = sem("xn_ready"), sem("xnT_ps"), sem("xnT_ready")
        qk_ps, vg_ps, qk_ready, vg_ready, g_ready = (sem(n) for n in (
            "qk_ps", "vg_ps", "qk_ready", "vg_ready", "g_ready"))
        s_ps, st_ready, av_ps, av_read, h2stat, r3_ready, h2_ready = (sem(n) for n in (
            "s_ps", "st_ready", "av_ps", "av_read", "h2stat", "r3_ready", "h2_ready"))
        xf_ready, x2T_ps, x2T_ready, lg_ps, th_ready, oh_ready = (sem(n) for n in (
            "xf_ready", "x2T_ps", "x2T_ready", "lg_ps", "th_ready", "oh_ready"))
        acc_ready, pos_ps, pos_read, slot_ready = (sem(n) for n in (
            "acc_ready", "pos_ps", "pos_read", "slot_ready"))
        sent = [sem(f"sent{n}") for n in range(XR)]
        dve_step, pool_step = sem("dve_step"), sem("pool_step")
        count_ps, list_ready = sem("count_ps"), sem("list_ready")
        xb_in = [sem(f"xb_in{n}") for n in range(NW + 1)]
        ew_in = [sem(f"ew_in{n}") for n in range(NW + 1)]
        xbT_ps, xbT_ready, gu_ps, gs_ready, hT_ready, ey_ps, ys_ready = (sem(n) for n in (
            "xbT_ps", "xbT_ready", "gu_ps", "gs_ready", "hT_ready", "ey_ps", "ys_ready"))
        put, put_over, put_late = [sem(f"put{n}") for n in range(NY)], sem("put_over"), sem("put_late")
        sh_ps, shg_ready, shT_ready, so_ps, so_ready = (sem(n) for n in (
            "sh_ps", "shg_ready", "shT_ready", "so_ps", "so_ready"))
        pr_in = [sem(f"pr_in{n}") for n in range(NS)]
        fin_ready, stored = sem("fin_ready"), sem("stored")

        block = ctx.enter_context(nc.Block())

        NB = NEG + 1
        OVER = NEG - NY

        def group(i):
            return i if i < OVER else i - 1

        def loaded(i):
            return (NW, EG) if i == OVER else (group(i) % NW, group(i) // NW + 1)

        def run_before(g):
            return g + 1 if g < OVER else g + 2

        def stores(i):
            return len(range(i % NY, min(i, OVER), NY))

        MORE = NOV // EG - 1
        LAST = NT + 5
        SHARED = [TG * (NG - 1) - 1 + p for p in range(LATE)]
        assert all(i >= TS * p + TS + 3 for p, i in enumerate(SHARED)) and SHARED[-1] + 1 < LAST
        FILLS = NE * CAP // P // FILLR
        SPARES = NOV * BLK // P // FILLR
        assert FILLS * FILLR * P == NE * CAP and SPARES * FILLR * P == NOV * BLK

        def first_blocks(g):
            return buf[g * EG * CAP:(g + 1) * EG * CAP].rearrange("(e s) w -> s e w", e=EG)[0:BLK]

        @block.sync
        def _(sp):
            def load_group(g):
                if g >= 2:
                    sp.wait_ge(conv_ps, g - 1)
                for n in range(NL):
                    if g == 0:
                        sp.dma_start(WP[:, n], wp[n]).then_inc(wp_in[n], 16)
                    sp.dma_start(X[:, g % 2, n * HC:(n + 1) * HC], xp[g, :, n * HC:(n + 1) * HC]
                                 ).then_inc(x_in[g % 2][n], 16)
                sp.dma_start(XE[:, g % 2], xe[g]).then_inc(x_in[g % 2][NL], 16)

            load_group(0)
            sp.dma_start(WE[:, :, :], we.rearrange("(c k) d -> k c d", k=2 * EDGE)).then_inc(we_in, 16)
            sp.dma_start(V[:, :], vecs).then_inc(v_in, 16)
            sp.dma_start(SQ[:, :], sq).then_inc(sq_in, 16)
            sp.dma_start(C[:, 0:NC_CONST - HEADS * P], cst[:, 0:NC_CONST - HEADS * P]).then_inc(c_in, 16)
            sp.dma_start(R[:, :], rows.partition_broadcast(P)).then_inc(r_in, 16)
            load_group(1)
            sp.dma_start(decay, cst[:, NC_CONST - HEADS * P:]).then_inc(decay_in, 16)
            sp.wait_ge(filled_tile, 1)
            main = buf[0:NE * CAP].rearrange("(p r) w -> p r w", p=P)
            spare = buf[NE * CAP:].rearrange("(p r) w -> p r w", p=P)
            for n in range(FILLS):
                if n == 3:
                    load_group(2)
                sp.dma_start(main[:, n * FILLR:(n + 1) * FILLR], fill[:, :, :]).then_inc(filled, 16)
            load_group(3)
            for n in range(SPARES):
                sp.dma_start(spare[:, n * FILLR:(n + 1) * FILLR], fill[:, :, :]).then_inc(spare_filled, 16)

            def load_weights(g):
                if g >= NW:
                    sp.wait_ge(ey_ps, run_before(g - NW))
                sp.dma_start(w13s[:, g % NW], w13[g * EG:(g + 1) * EG].rearrange("e d n -> d e n")
                             ).then_inc(ew_in[g % NW], 16)
                sp.dma_start(w2s[HID:P, g % NW], w2[g * EG:(g + 1) * EG].rearrange("e d n -> d e n")
                             ).then_inc(ew_in[g % NW], 16)

            def load_rows(g):
                if g >= NW:
                    sp.wait_ge(xbT_ps, run_before(g - NW))
                sp.dma_start(xb[:, g % NW], first_blocks(g)).then_inc(xb_in[g % NW], 16)

            def load_overflow(n, e):
                row = sp.value_load(ovrow[0:1, bass.ds(n * EG + e, 1)], min_val=0,
                                    max_val=NE * CAP + (NOV - 1) * BLK)
                sp.dma_start(xb[:, NW, e], buf[bass.ds(row, BLK), :]).then_inc(xb_in[NW], 16)
                exp = sp.value_load(ovexp[0:1, bass.ds(n * EG + e, 1)], min_val=0, max_val=NE - 1)
                sp.dma_start(w13s[:, NW, e],
                             w13[bass.ds(exp, 1)].rearrange("e d n -> (e d) n")).then_inc(ew_in[NW], 16)
                sp.dma_start(w2s[HID:P, NW, e],
                             w2[bass.ds(exp, 1)].rearrange("e d n -> (e d) n")).then_inc(ew_in[NW], 16)

            def store_overflow(n, q):
                z = q % NY if q < NB else 0
                sp.wait_ge(ys_ready, q + 1)
                for e in range(EG):
                    row = sp.value_load(ovrow[0:1, bass.ds(n * EG + e, 1)], min_val=0,
                                        max_val=NE * CAP + (NOV - 1) * BLK)
                    sp.dma_start(buf[bass.ds(row, BLK), :], ys[:, z, e]).then_inc(put_over, 16)

            for q in range(NW):
                load_weights(q)
            for n in range(XR):
                sp.wait_ge(sent[n], 16 * TOPK * (NT // XR))
            for q in range(NW):
                load_rows(q)
            sp.wait_ge(list_ready, 1)
            sp.wait_ge(spare_filled, 16 * SPARES)
            for g in range(NW, NEG):
                if (g - NW) % 2 == 0 and (g - NW) // 2 < EG:
                    load_overflow(0, (g - NW) // 2)
                load_weights(g)
                load_rows(g)
            store_overflow(0, OVER)
            for q in range(OVER + 1, NB):
                sp.wait_ge(ys_ready, q + 1)
                sp.dma_start(first_blocks(group(q)), ys[:, q % NY]).then_inc(put_late, 16)
            more = sp.value_load(ovn[0:1, 0:1], min_val=0, max_val=NOV // EG - 1)
            for n in range(MORE):
                with sp.If(more > n):
                    sp.wait_ge(ey_ps, NB + n)
                    for e in range(EG):
                        load_overflow(n + 1, e)
                    store_overflow(n + 1, NB + n)
            ov = out.rearrange("(t p) d -> p t d", p=P)
            for p in range(NS):
                sp.wait_ge(fin_ready, p + 1)
                sp.dma_start(ov[:, p * TS:(p + 1) * TS], h[:, p * TS:(p + 1) * TS]).then_inc(stored, 16)
            sp.wait_ge(stored, 16 * NS)

        @block.tensor
        def _(pe):
            def conv(g, j):
                if j % HC == 0:
                    pe.wait_ge(x_in[g % 2][j // HC], 16 * (g // 2 + 1))
                    if g == 0 and j < NCH:
                        pe.wait_ge(w_ready, j // HC + 1)
                    if g == 0 and j == NCH:
                        pe.wait_ge(we_in, 16)
                if j == 0 and g >= 1:
                    pe.wait_ge(yT_ready, g)
                if j < NCH:
                    w, x = W[:, j], X[:, g % 2, j]
                else:
                    w, x = WE[:, j - NCH], XE[:, g % 2, j - NCH]
                mm = nc.tensor.matmul(CONV[:, :], w, x, start=(j == 0), stop=(j == NCH + 1))
                if j == NCH + 1:
                    mm.then_inc(conv_ps, 1)

            def embed(t):
                pe.wait_ge(yT_ready, t // TG + 1)
                if t >= 1:
                    pe.wait_ge(h_ready, t)
                y = yT[:, t // TG % 2, t % TG * P:(t % TG + 1) * P]
                nc.tensor.transpose(A[:, 0:P], y, ident)
                nc.tensor.matmul(A[:, P:2 * P], y, WD[:, :], start=True, stop=True).then_inc(y_ps, 1)

            def turn_xn(t):
                pe.wait_ge(xn_ready, t + 1)
                if t >= 4:
                    pe.wait_ge(x2T_ready, t - 3)
                nc.tensor.transpose(TR[:, 0:P], xn[:, t % 2], ident).then_inc(xnT_ps, 1)

            def project(t):
                pe.wait_ge(xnT_ready, t + 1)
                if t >= 1:
                    pe.wait_ge(qk_ready, t)
                nc.tensor.matmul(QK[:, 0:P], wq, xnT[:, t % 2], start=True, stop=True)
                nc.tensor.matmul(QK[:, P:2 * P], wk, xnT[:, t % 2], start=True, stop=True).then_inc(qk_ps, 1)
                if t >= 1:
                    pe.wait_ge(vg_ready, t)
                nc.tensor.matmul(VG[:, 0:2 * P], xnT[:, t % 2], wvg, start=True, stop=True).then_inc(vg_ps, 1)

            def scores(t):
                pe.wait_ge(qk_ready, t + 1)
                if t >= 1:
                    pe.wait_ge(st_ready, 2 * t)
                for n, s in enumerate((S0, S1)):
                    mm = nc.tensor.matmul(s[:, :], kT[:, t % 2, n], qm[:, t % 2].rearrange("p a i -> p (a i)"),
                                          start=True, stop=True)
                mm.then_inc(s_ps, 1)

            def attend(t, n):
                if n == 0:
                    pe.wait_ge(vg_ready, t + 1)
                    if t >= 2:
                        pe.wait_ge(th_ready, t - 1)
                pe.wait_ge(st_ready, 2 * t + n + 1)
                for hh in range(n * QM, (n + 1) * QM):
                    mm = nc.tensor.matmul(O[:, hh * HD:(hh + 1) * HD], ST[:, t % 2, hh],
                                          vg[:, t % 4, hh * HD:(hh + 1) * HD], start=True, stop=True)
                if n == 1:
                    mm.then_inc(av_ps, 1)

            def places(t):
                pe.wait_ge(oh_ready, t + 1)
                if t == 0:
                    pe.wait_ge(before_ready, 1)
                    pe.wait_ge(ones_set, 1)
                if t >= 1:
                    pe.wait_ge(acc_ready, t)
                pe.wait_ge(av_read, min(t + 3, NT))
                pe.wait_ge(th_ready, t + 1)
                for k in range(TOPK):
                    mm = nc.tensor.matmul(O[:, 0:NE], before[:, :], OH[:, t % 4, k],
                                          start=(k == 0), stop=(t == 0 and k == TOPK - 1))
                if t >= 1:
                    mm = nc.tensor.matmul(O[:, 0:NE], ones[:, :], acc[:, t % 3], start=False, stop=True)
                mm.then_inc(pos_ps, 1)

            def turn_xf(t):
                pe.wait_ge(xf_ready, t + 1)
                pe.wait_ge(xnT_ready, min(t + 4, NT))
                nc.tensor.transpose(TR[:, 0:P], xrow[:, t % XR], ident).then_inc(x2T_ps, 1)

            def logits(t):
                pe.wait_ge(x2T_ready, t + 1)
                if t >= 1:
                    pe.wait_ge(pos_read, t)
                pe.wait_ge(av_read, min(t + 2, NT))
                nc.tensor.matmul(O[:, 0:NE], x2T[:, t], gw, start=True, stop=True).then_inc(lg_ps, 1)

            def shared_up(p):
                pe.wait_ge(x2T_ready, TS * (p + 1))
                if p == 0:
                    pe.wait_ge(yT_ready, NG)
                else:
                    pe.wait_ge(so_ready, p)
                x = x2T[:, p * TS:(p + 1) * TS].rearrange("p t n -> p (t n)")
                nc.tensor.matmul(SH1, s1, x, start=True, stop=True)
                nc.tensor.matmul(SH3, s3, x, start=True, stop=True).then_inc(sh_ps, 1)

            def shared_down(p):
                pe.wait_ge(shT_ready, p + 1)
                for n in range(TS):
                    mm = nc.tensor.matmul(SH1[:, n * P:(n + 1) * P], shT[:, n], s2, start=True, stop=True)
                mm.then_inc(so_ps, 1)

            for j in range(NCH + 2):
                conv(0, j)
            pe.wait_ge(c_in, 16)
            pe.wait_ge(sq_in, 16)
            pe.wait_ge(wd_in_ready, 1)
            nc.tensor.matmul(QK[:, 0:P], center, gdw[:, :], start=True, stop=True)
            nc.tensor.matmul(VG[:, 0:P], betab[:, :], dw, start=True, stop=True).then_inc(wd_ps, 1)
            pe.wait_ge(wd_ready, 1)
            pe.wait_ge(cvec_ready, 1)

            def conv_step(i, n):
                g, j = (i + 1) // TG + 1, 2 * ((i + 1) % TG) + n
                if i == 0:
                    conv(g, n)
                if g < NG:
                    conv(g, j)

            embed(0)
            for i in range(LAST):
                if 0 <= i - 2 < NT:
                    scores(i - 2)
                if 0 <= i - 4 < NT:
                    turn_xf(i - 4)
                if 0 <= i - 3 < NT:
                    attend(i - 3, 0)
                if i - 1 in SHARED:
                    shared_down(SHARED.index(i - 1))
                if 0 <= i - 1 < NT:
                    project(i - 1)
                if 0 <= i - 3 < NT:
                    attend(i - 3, 1)
                conv_step(i, 0)
                if i in SHARED:
                    shared_up(SHARED.index(i))
                if i < NT:
                    turn_xn(i)
                if 0 <= i - 5 < NT:
                    places(i - 5)
                if i + 1 < NT:
                    embed(i + 1)
                conv_step(i, 1)
                if 0 <= i - 4 < NT:
                    logits(i - 4)
            pe.wait_ge(acc_ready, NT)
            pe.wait_ge(pos_read, NT)
            nc.tensor.matmul(O[:, 0:NE], ones[:, :], acc[:, NT % 3], start=True, stop=True).then_inc(count_ps, 1)

            def turn_rows(q, u, v=0, first=False, back=2):
                if not first:
                    pe.wait_ge(xbT_ready, q - back + 1)
                for e in range(EG):
                    mm = nc.tensor.transpose(XT[u][:, e * BLK:(e + 1) * BLK], xb[:, v, e], ident)
                mm.then_inc(xbT_ps, 1)

            def gate_up(q, u, v=0, first=False, back=2):
                if not first:
                    pe.wait_ge(hT_ready, q - back + 1)
                pe.wait_ge(xbT_ready, q + 1)
                for e in range(EG):
                    mm = nc.tensor.matmul(GU[u][:, e * BLK:(e + 1) * BLK], w13s[:, v, e], xbT[:, u, e],
                                          start=True, stop=True)
                mm.then_inc(gu_ps, 1)

            def down(q, u, v=0, first=False, back=2):
                if not first:
                    pe.wait_ge(ys_ready, q - back + 1)
                pe.wait_ge(hT_ready, q + 1)
                for e in range(EG):
                    mm = nc.tensor.matmul(Y[u][:, e * P:(e + 1) * P], hT[HID:P, u, e], w2s[HID:P, v, e],
                                          start=True, stop=True)
                mm.then_inc(ey_ps, 1)

            for i in range(NB + 2):
                if i < NB:
                    v, uses = loaded(i)
                    pe.wait_ge(xb_in[v], 16 * uses)
                    turn_rows(i, i % 2, v, first=i < 2)
                if 0 <= i - 1 < NB:
                    q = i - 1
                    v, uses = loaded(q)
                    pe.wait_ge(ew_in[v], 32 * uses)
                    gate_up(q, q % 2, v, first=q < 2)
                if 0 <= i - 2 < NB:
                    down(i - 2, (i - 2) % 2, loaded(i - 2)[0], first=i - 2 < 2)
            for p in range(LATE, NS):
                shared_up(p)
                shared_down(p)
            more = pe.value_load(ovn[0:1, 0:1], min_val=0, max_val=NOV // EG - 1)
            for n in range(MORE):
                with pe.If(more > n):
                    pe.wait_ge(xb_in[NW], 16 * EG * (n + 2))
                    pe.wait_ge(ew_in[NW], 32 * EG * (n + 2))
                    turn_rows(n + NB, 0, NW, back=1)
                    gate_up(n + NB, 0, NW, back=1)
                    down(n + NB, 0, NW, back=1)

        @block.scalar
        def _(act):
            def evac_y(g):
                act.wait_ge(conv_ps, g + 1)
                if g == 0:
                    act.wait_ge(v_in, 16)
                if g >= 2:
                    act.wait_ge(y_ps, TG * (g - 1))
                nc.scalar.activation(yT[:, g % 2].rearrange("d (b p) -> d b p", p=T),
                                     CONV[:, :].rearrange("d (p b) -> d b p", p=T),
                                     ACT.Identity, bias=conv_b).then_inc(yT_ready, 1)

            def evac_xn(t):
                act.wait_ge(xnT_ps, t + 1)
                if t >= 2:
                    act.wait_ge(vg_ps, t - 1)
                nc.scalar.activation(xnT[:, t % 2], TR[:, 0:P], ACT.Copy).then_inc(xnT_ready, 1)

            def evac_qk(t):
                act.wait_ge(qk_ps, t + 1)
                if t == 0:
                    act.wait_ge(bqm_ready, 1)
                    act.wait_ge(kT_zeroed, 1)
                if t >= 2:
                    act.wait_ge(s_ps, t - 1)
                for m in range(QM):
                    nc.scalar.activation(qm[:, t % 2, m], QK[:, 0:P], ACT.Identity,
                                         bias=bqm[:, m:m + 1], scale=head[:, m:m + 1])
                for n in range(2):
                    own = slice(n * P // 2, (n + 1) * P // 2)
                    ins = nc.scalar.activation(kT[own, t % 2, n], QK[own, P:2 * P], ACT.Identity, bias=bk[own])
                ins.then_inc(qk_ready, 1)

            def gates(t):
                act.wait_ge(vg_ready, t + 1)
                nc.scalar.activation(vg[:, t % 4, P:2 * P], vg[:, t % 4, P:2 * P], ACT.Silu).then_inc(g_ready, 1)

            def evac_xf(t):
                act.wait_ge(x2T_ps, t + 1)
                nc.scalar.activation(x2T[:, t], TR[:, 0:P], ACT.Copy).then_inc(x2T_ready, 1)

            def tanhs(t):
                act.wait_ge(lg_ps, t + 1)
                if t >= 2:
                    act.wait_ge(oh_ready, t - 1)
                nc.scalar.activation(th[:, t % 2], O[:, 0:NE], ACT.Tanh, scale=0.5).then_inc(th_ready, 1)

            def shared_gate(p):
                act.wait_ge(sh_ps, p + 1)
                if p >= 1:
                    act.wait_ge(shT_ready, p)
                nc.scalar.activation(shg[:, :], SH1, ACT.Silu).then_inc(shg_ready, 1)

            evac_y(0)
            act.wait_ge(wd_ps, 1)
            nc.scalar.activation(WD[:, :], QK[:, 0:P], ACT.Copy).then_inc(wd_ready, 1)
            for i in range(LAST):
                if 0 <= i - 4 < NT:
                    evac_xf(i - 4)
                if 0 <= i - 1 < NT:
                    evac_qk(i - 1)
                    gates(i - 1)
                if i in SHARED:
                    shared_gate(SHARED.index(i))
                if i < NT:
                    evac_xn(i)
                if i % TG == 2 and i // TG + 1 < NG:
                    evac_y(i // TG + 1)
                if 0 <= i - 4 < NT:
                    tanhs(i - 4)

            def evac_rows(q, u, v=0, first=False, back=2):
                act.wait_ge(xbT_ps, q + 1)
                if not first:
                    act.wait_ge(gu_ps, q - back + 1)
                nc.scalar.activation(xbT[:, u].rearrange("p e s -> p (e s)"), XT[u][:, :], ACT.Copy
                                     ).then_inc(xbT_ready, 1)

            def gate(q, u, v=0, first=False, back=2):
                act.wait_ge(gu_ps, q + 1)
                if not first:
                    act.wait_ge(hT_ready, q - back + 1)
                nc.scalar.activation(gs[HID:P, u], GU[u][0:HID, :], ACT.Silu).then_inc(gs_ready, 1)

            for i in range(NB + 1):
                if i < NB:
                    evac_rows(i, i % 2, first=i < 2)
                if 0 <= i - 1 < NB:
                    gate(i - 1, (i - 1) % 2, first=i - 1 < 2)
            for p in range(LATE, NS):
                shared_gate(p)
            more = act.value_load(ovn[0:1, 0:1], min_val=0, max_val=NOV // EG - 1)
            for n in range(MORE):
                with act.If(more > n):
                    evac_rows(n + NB, 0, back=1)
                    gate(n + NB, 0, back=1)

        @block.vector
        def _(dve):
            steps = [0]

            def own(ins):
                steps[0] += 1
                ins.then_inc(dve_step, 1)
                dve.wait_ge(dve_step, steps[0])

            for n in range(NL):
                dve.wait_ge(wp_in[n], 16)
                c = slice(n * HC, (n + 1) * HC)
                own(nc.vector.tensor_tensor(W[:, c], WP[:, n, 0], WP[:, n, 1], ALU.add))
                for s in range(2, 5):
                    ins = nc.vector.tensor_tensor(W[:, c], W[:, c], WP[:, n, s], ALU.add)
                    if s == 4:
                        ins.then_inc(w_ready, 1)
                    else:
                        own(ins)
            dve.wait_ge(v_in, 16)
            dve.wait_ge(sq_in, 16)
            nc.vector.tensor_scalar(gdw[:, :], dw, gamma, None, ALU.mult)
            nc.vector.tensor_copy(betab[:, :], beta.to_broadcast([P, P])).then_inc(wd_in_ready, 1)
            dve.wait_ge(c_in, 16)
            nc.vector.tensor_copy(before[:, :], before_f).then_inc(before_ready, 1)
            nc.vector.tensor_scalar(bqm[:, :], head, bq, None, ALU.mult).then_inc(bqm_ready, 1)
            dve.wait_ge(r_in, 16)
            dve.wait_ge(wd_ps, 1)
            nc.vector.tensor_tensor(cvec[:, :], VG[:, 0:P], dense_bias, ALU.add).then_inc(cvec_ready, 1)

            def step(ins):
                steps[0] += 1
                ins.then_inc(dve_step, 1)
                return steps[0]

            def head_steps(i):
                y, c = i < NT, 0 <= i - 5 < NT
                t, u = i, i - 5
                if y:
                    dve.wait_ge(y_ps, t + 1)
                    y1 = step(nc.vector.bn_stats(st1[:, t % 2], A[:, 0:P]))
                if c:
                    dve.wait_ge(th_ready, u + 1)
                    c1 = step(nc.vector.tensor_scalar(sg[:, :], th[:, u % 2], 0.5, 0.5, ALU.mult, ALU.add))
                if y:
                    dve.wait_ge(dve_step, y1)
                    nc.vector.bn_aggr(mv1[:, t % 2], st1[:, t % 2]).then_inc(ystat, 1)
                if c:
                    dve.wait_ge(dve_step, c1)
                    c2 = step(nc.vector.max(top[:, :], sg[:, :]))
                    dve.wait_ge(dve_step, c2)
                    c3 = step(nc.vector.max_index(topi[:, :], top[:, :], sg[:, :]))
                    c6 = step(nc.vector.tensor_scalar(ssum[:, :], top[:, 0:1], top[:, 1:2], 1e-20,
                                                      ALU.add, ALU.add))
                    dve.wait_ge(dve_step, c3)
                    c4 = step(nc.vector.tensor_copy(idx[:, u % 4], topi[:, 0:TOPK]))
                    dve.wait_ge(dve_step, c6)
                    c7 = step(nc.vector.reciprocal(srec[:, :], ssum[:, :]))
                    if u >= 4:
                        dve.wait_ge(pos_ps, u - 3)
                        dve.wait_ge(acc_ready, u - 3)
                    dve.wait_ge(dve_step, c4)
                    nc.vector.tensor_tensor(OH[:, u % 4], expert.unsqueeze(1).broadcast_to([P, TOPK, NE]),
                                            idx[:, u % 4].unsqueeze(2).broadcast_to([P, TOPK, NE]),
                                            ALU.is_equal).then_inc(oh_ready, 1)
                    dve.wait_ge(dve_step, c7)
                    nc.vector.tensor_scalar(pw[:, u], top[:, 0:TOPK], srec[:, 0:1], ROUTE_SCALE,
                                            ALU.mult, ALU.mult)
                if y:
                    dve.wait_ge(r1_ready, t + 1)
                    if t == 0:
                        dve.wait_ge(cvec_ready, 1)
                    nc.vector.scalar_tensor_tensor(out=h[:, t], in0=A[:, P:2 * P], scalar=rs1[:, t % 2],
                                                   in1=cvec[:, :], op0=ALU.mult, op1=ALU.add).then_inc(h_ready, 1)
                if y:
                    dve.wait_ge(h_ready, t + 1)
                    h2 = step(nc.vector.bn_stats(st2[:, t % 2], h[:, t]))
                if y:
                    dve.wait_ge(dve_step, h2)
                    nc.vector.bn_aggr(mv2[:, t % 2], st2[:, t % 2]).then_inc(hstat, 1)

            def middle_steps(i):
                a, f = 0 <= i - 3 < NT, 0 <= i - 5 < NT
                t, u = i - 3, i - 5
                if a:
                    dve.wait_ge(av_ps, t + 1)
                    dve.wait_ge(g_ready, t + 1)
                    nc.vector.tensor_tensor(go[:, :], O[:, 0:P], vg[:, t % 4, P:2 * P], ALU.mult
                                            ).then_inc(av_read, 1)
                if a:
                    dve.wait_ge(av_read, t + 1)
                    nc.vector.tensor_tensor(h[:, t], h[:, t], go[:, :], ALU.add).then_inc(h2_ready, 1)
                if f:
                    dve.wait_ge(pos_ps, u + 1)
                    nc.vector.tensor_tensor(mpos[:, :, :], O[:, 0:NE].unsqueeze(1).broadcast_to([P, TOPK, NE]),
                                            OH[:, u % 4], ALU.mult).then_inc(pos_read, 1)
                if f:
                    dve.wait_ge(pos_read, u + 1)
                    f2 = step(nc.vector.tensor_reduce(pos[:, :], mpos[:, :, :], AX.X, ALU.add))
                if a:
                    dve.wait_ge(h2_ready, t + 1)
                    a3 = step(nc.vector.bn_stats(st3[:, t % 2], h[:, t]))
                if f:
                    dve.wait_ge(dve_step, f2)
                    step(nc.vector.tensor_scalar(over[:, :], pos[:, :], CAP - 0.5, float(BIG),
                                                 ALU.is_gt, ALU.mult))
                    f4 = step(nc.vector.scalar_tensor_tensor(out=place[:, :], in0=idx[:, u % 4],
                                                             scalar=float(CAP), in1=pos[:, :],
                                                             op0=ALU.mult, op1=ALU.add))
                if a:
                    dve.wait_ge(dve_step, a3)
                    nc.vector.bn_aggr(mv3[:, t % 2], st3[:, t % 2]).then_inc(h2stat, 1)
                if f:
                    dve.wait_ge(dve_step, f4)
                    nc.vector.tensor_tensor(slots[:, :, u], over[:, :], place[:, :], ALU.add).then_inc(slot_ready, 1)

            def bias_vg(t):
                dve.wait_ge(vg_ps, t + 1)
                if t >= 4:
                    dve.wait_ge(av_ps, t - 3)
                nc.vector.tensor_tensor(vg[:, t % 4], VG[:, 0:2 * P], vg_bias, ALU.add).then_inc(vg_ready, 1)

            def norm_h(t):
                dve.wait_ge(r2_ready, t + 1)
                if t >= 2:
                    dve.wait_ge(xnT_ps, t - 1)
                nc.vector.tensor_scalar(xn[:, t % 2], h[:, t], mv2[:, t % 2, 0:1], rs2[:, t % 2],
                                        ALU.subtract, ALU.mult).then_inc(xn_ready, 1)

            def norm_h2(t):
                dve.wait_ge(r3_ready, t + 1)
                if t >= XR:
                    dve.wait_ge(sent[t % XR], 16 * TOPK * (t // XR))
                    dve.wait_ge(x2T_ps, t - XR + 1)
                nc.vector.tensor_scalar(xrow[:, t % XR], h[:, t], mv3[:, t % 2, 0:1], rs3[:, t % 2],
                                        ALU.subtract, ALU.mult).then_inc(xf_ready, 1)

            def decay_scores(t):
                dve.wait_ge(s_ps, t + 1)
                if t == 0:
                    dve.wait_ge(decay_in, 16)
                if t >= 2:
                    dve.wait_ge(av_ps, t - 1)
                for n, s in enumerate((S0, S1)):
                    nc.vector.tensor_tensor(
                        ST[:, t % 2, n * QM:(n + 1) * QM].rearrange("p a i -> p (a i)"), s[:, :],
                        decay[:, n * 512:(n + 1) * 512], ALU.mult).then_inc(st_ready, 1)

            def shared_hidden(p):
                dve.wait_ge(shg_ready, p + 1)
                if p >= 1:
                    dve.wait_ge(so_ps, p)
                nc.vector.tensor_tensor(shT[:, :].rearrange("p t n -> p (t n)"), SH3, shg[:, :],
                                        ALU.mult).then_inc(shT_ready, 1)

            def shared_add(p):
                dve.wait_ge(so_ps, p + 1)
                hp = h[:, p * TS:(p + 1) * TS].rearrange("p t n -> p (t n)")
                nc.vector.tensor_tensor(hp, SH1, hp, ALU.add).then_inc(so_ready, 1)

            for i in range(LAST):
                head_steps(i)
                if 0 <= i - 2 < NT:
                    decay_scores(i - 2)
                if i - 1 in SHARED:
                    shared_add(SHARED.index(i - 1))
                if i < NT:
                    norm_h(i)
                if 0 <= i - 1 < NT:
                    bias_vg(i - 1)
                middle_steps(i)
                if i in SHARED:
                    shared_hidden(SHARED.index(i))
                if 0 <= i - 3 < NT:
                    norm_h2(i - 3)

            dve.wait_ge(count_ps, 1)
            own(nc.vector.scalar_tensor_tensor(out=ovv[:, :], in0=O[:, 0:NE], scalar=BLK + 0.5, in1=left,
                                               op0=ALU.is_gt, op1=ALU.mult))
            for n in range(NOV // 8):
                src, dst = (ovv, ovw) if n % 2 == 0 else (ovw, ovv)
                own(nc.vector.max(ovl[:, 8 * n:8 * n + 8], src[:, :]))
                if n < NOV // 8 - 1:
                    own(nc.vector.match_replace(dst[:, :], ovl[:, 8 * n:8 * n + 8], src[:, :], 0.0))
            own(nc.vector.tensor_scalar(ovf[:, :], ovl[:, :], -1.0, float(NE), ALU.mult, ALU.add))
            nc.vector.tensor_scalar(ovm[:, :], ovl[:, :], 0.5, None, ALU.is_gt)
            own(nc.vector.tensor_scalar(ova[:, :], expert[:, 0:NOV], -1.0, -float(BLK), ALU.add, ALU.mult))
            own(nc.vector.tensor_tensor(ovm[:, :], ovm[:, :], ova[:, :], ALU.mult))
            own(nc.vector.scalar_tensor_tensor(out=ovm[:, :], in0=expert[:, 0:NOV], scalar=float(BLK),
                                               in1=ovm[:, :], op0=ALU.mult, op1=ALU.add))
            nc.vector.scalar_tensor_tensor(out=ovrow[:, :], in0=ovf[:, :], scalar=float(CAP),
                                           in1=ovm[:, :], op0=ALU.mult, op1=ALU.add)
            nc.vector.tensor_scalar(ovexp[:, :], ovf[:, :], float(NE - 1), None, ALU.min)
            own(nc.vector.tensor_scalar(ovc[:, :], ovl[:, ::EG], 0.5, None, ALU.is_gt))
            own(nc.vector.tensor_reduce(ovs[:, :], ovc[:, 1:], AX.X, ALU.add))
            nc.vector.tensor_copy(ovn[:, :], ovs[:, :]).then_inc(list_ready, 1)

            def hidden(q, u, v=0, first=False, back=2):
                dve.wait_ge(gs_ready, q + 1)
                if not first:
                    dve.wait_ge(ey_ps, q - back + 1)
                nc.vector.tensor_tensor(hT[HID:P, u].rearrange("p e s -> p (e s)"), GU[u][HID:P, :],
                                        gs[HID:P, u], ALU.mult).then_inc(hT_ready, 1)

            def evac_out(q, u):
                dve.wait_ge(ey_ps, q + 1)
                z = q % NY if q < NB else 0
                if q >= NY:
                    dve.wait_ge(put[z], 16 * (stores(q) if q < NB else stores(NY * NB)))
                if q >= NB:
                    dve.wait_ge(put_late, 16 * (NB - 1 - OVER))
                if q >= NB or q == OVER + NY:
                    dve.wait_ge(put_over, 16 * EG * max(q - NB + 1, 1))
                nc.vector.tensor_copy(ys[:, z].rearrange("p e n -> p (e n)"), Y[u][:, :]).then_inc(ys_ready, 1)

            for i in range(NB + 2):
                if 0 <= i - 1 < NB:
                    hidden(i - 1, (i - 1) % 2, first=i - 1 < 2)
                if 0 <= i - 2 < NB:
                    evac_out(i - 2, (i - 2) % 2)
            for p in range(LATE, NS):
                shared_hidden(p)
                shared_add(p)
            more = dve.value_load(ovn[0:1, 0:1], min_val=0, max_val=NOV // EG - 1)
            for n in range(MORE):
                with dve.If(more > n):
                    hidden(n + NB, 0, back=1)
                    evac_out(n + NB, 0)

            for p in range(NS):
                dve.wait_ge(pr_in[p], 16 * TOPK * TS)
                dve.wait_ge(so_ready, p + 1)
                for k in range(TOPK):
                    for t in range(p * TS, (p + 1) * TS):
                        ins = nc.vector.scalar_tensor_tensor(out=h[:, t], in0=pr[:, t, k], scalar=pw[:, t, k:k + 1],
                                                             in1=h[:, t], op0=ALU.mult, op1=ALU.add)
                        if k < TOPK - 1:
                            last = step(ins)
                    if k < TOPK - 1:
                        dve.wait_ge(dve_step, last)
                ins.then_inc(fin_ready, 1)

        @block.gpsimd
        def _(pool):
            steps = [0]

            def own(ins):
                steps[0] += 1
                ins.then_inc(pool_step, 1)
                pool.wait_ge(pool_step, steps[0])

            pool.memset(kT[:, :, :, :], 0.0).then_inc(kT_zeroed, 1)
            pool.memset(fill[:, :, :], 0.0).then_inc(filled_tile, 1)
            pool.memset(mhalf[:, :], -0.5)
            pool.memset(acc[:, 0], 0.0)
            own(pool.memset(ones[:, :], 1.0))
            pool.sem_inc(ones_set, 1)

            def rstd(t, stat, eps, mv, ve, rs, ready):
                pool.wait_ge(stat, t + 1)
                own(pool.tensor_scalar(ve[:, t % 2], mv[:, t % 2, 1:2], 1.0, eps, ALU.mult, ALU.add))
                pool.tensor_tensor(rs[:, t % 2], ve[:, t % 2], mhalf[:, :], ALU.pow).then_inc(ready, 1)

            def accumulate(t):
                pool.wait_ge(oh_ready, t + 1)
                if t >= 2:
                    pool.wait_ge(pos_ps, t - 1)
                own(pool.tensor_tensor(acc[:, (t + 1) % 3], acc[:, t % 3], OH[:, t % 4, 0], ALU.add))
                pool.tensor_tensor(acc[:, (t + 1) % 3], acc[:, (t + 1) % 3], OH[:, t % 4, 1], ALU.add
                                   ).then_inc(acc_ready, 1)
                pool.wait_ge(acc_ready, t + 1)

            def send(t, k):
                pool.wait_ge(slot_ready, t + 1)
                pool.wait_ge(xf_ready, t + 1)
                if t == 0:
                    pool.wait_ge(filled, 16 * FILLS)
                pool.indirect_dma_start(
                    buf, bass.IndirectOffsetOnAxis(ap=slots[:, k, t:t + 1], axis=0),
                    xrow[:, t % XR], None, bounds_check=NE * CAP - 1, oob_is_err=False
                ).then_inc(sent[t % XR], 16)

            for i in range(LAST):
                if i < NT:
                    rstd(i, ystat, LN_TOK, mv1, ve1, rs1, r1_ready)
                if 0 <= i - 6 < NT:
                    send(i - 6, 0)
                if 0 <= i - 5 < NT:
                    accumulate(i - 5)
                if i < NT:
                    rstd(i, hstat, LN, mv2, ve2, rs2, r2_ready)
                if 0 <= i - 6 < NT:
                    send(i - 6, 1)
                if 0 <= i - 3 < NT:
                    rstd(i - 3, h2stat, LN, mv3, ve3, rs3, r3_ready)
            for k in range(TOPK):
                send(NT - 1, k)

            pool.wait_ge(conv_ps, NG)
            pool.memset(pr[:, :, :, :], 0.0).then_inc(pr_zeroed, 1)

            for q in range(OVER):
                pool.wait_ge(ys_ready, q + 1)
                pool.dma_start(first_blocks(group(q)), ys[:, q % NY]).then_inc(put[q % NY], 16)
            more = pool.value_load(ovn[0:1, 0:1], min_val=0, max_val=NOV // EG - 1)
            for n in range(MORE):
                with pool.If(more > n):
                    pool.wait_ge(put_over, 16 * EG * (n + 2))
            pool.wait_ge(put_over, 16 * EG)
            pool.wait_ge(put_late, 16 * (NB - 1 - OVER))
            for z in range(NY):
                pool.wait_ge(put[z], 16 * stores(NY * NB + z))
            pool.wait_ge(pr_zeroed, 1)
            for t in range(NT):
                for k in range(TOPK):
                    pool.indirect_dma_start(
                        pr[:, t, k], None, buf,
                        bass.IndirectOffsetOnAxis(ap=slots[:, k, t:t + 1], axis=0),
                        bounds_check=NE * CAP - 1, oob_is_err=False).then_inc(pr_in[t // TS], 16)


def kernel(x, L0_tok_conv_w, L0_tok_conv_b, L0_tok_gamma, L0_tok_beta, L0_tok_dense_w, L0_tok_dense_b,
           L0_attn_wq, L0_attn_bq, L0_attn_wk, L0_attn_bk, L0_attn_wv, L0_attn_bv, L0_attn_wg, L0_attn_bg,
           L0_ffn_gate_w, L0_ffn_w1, L0_ffn_w3, L0_ffn_w2, L0_ffn_sw1, L0_ffn_sw3, L0_ffn_sw2):
    import concourse.bacc as bacc
    from concourse.bass_utils import run_bass_kernel_spmd

    x = np.asarray(x)
    img = x.reshape(NG, GB, GRID, PATCH, GRID, PATCH, CH).transpose(0, 3, 5, 6, 2, 4, 1)
    xp = np.ascontiguousarray(img).reshape(NG, NCH, P, GN).transpose(0, 2, 1, 3)
    xe = np.zeros((NG, 4, EDGE, GRID, GRID, GB), x.dtype)
    xe[:, 0, :, 1:] = img[:, PATCH - 1].reshape(NG, EDGE, GRID, GRID, GB)[:, :, :-1]
    xe[:, 1, :, :-1] = img[:, 0].reshape(NG, EDGE, GRID, GRID, GB)[:, :, 1:]
    xe[:, 2, :, :, 1:] = img[:, :, PATCH - 1].reshape(NG, EDGE, GRID, GRID, GB)[:, :, :, :-1]
    xe[:, 3, :, :, :-1] = img[:, :, 0].reshape(NG, EDGE, GRID, GRID, GB)[:, :, :, 1:]
    xe = xe.reshape(NG, 2, 2 * EDGE, GN).transpose(0, 2, 1, 3)

    cw = np.asarray(L0_tok_conv_w).reshape(PATCH, PATCH, 5, CH, P)
    wp = np.zeros((5, PATCH, PATCH, CH, P), cw.dtype)
    wp[0] = cw[:, :, 0]
    wp[1, :, :-1] = cw[:, 1:, 1]
    wp[2, :, 1:] = cw[:, :-1, 2]
    wp[3, :-1] = cw[1:, :, 3]
    wp[4, 1:] = cw[:-1, :, 4]
    wp = wp.reshape(5, NL, HC, P, P).transpose(1, 3, 0, 2, 4)
    we = np.concatenate([cw[0, :, 3].reshape(EDGE, P), cw[PATCH - 1, :, 4].reshape(EDGE, P),
                         cw[:, 0, 1].reshape(EDGE, P), cw[:, PATCH - 1, 2].reshape(EDGE, P)])

    sq = np.concatenate([np.asarray(L0_tok_dense_w), np.asarray(L0_attn_wq).T, np.asarray(L0_attn_wk).T,
                         np.asarray(L0_attn_wv).T, np.asarray(L0_attn_wg).T, np.asarray(L0_ffn_sw1),
                         np.asarray(L0_ffn_sw3), np.asarray(L0_ffn_sw2), np.asarray(L0_ffn_gate_w).T], 1)
    w13 = np.concatenate([np.asarray(L0_ffn_w1), np.asarray(L0_ffn_w3)], 2)
    vecs = np.stack([np.asarray(v) for v in (L0_tok_conv_b, L0_tok_gamma, L0_tok_beta, L0_attn_bq, L0_attn_bk)], 1)
    rows = np.concatenate([np.asarray(L0_attn_bv), np.asarray(L0_attn_bg), np.asarray(L0_tok_dense_b)])
    cst = constants()

    nc = bacc.Bacc("TRN2", target_bir_lowering=False, num_devices=1)
    arrays, args = {}, []
    for name, a in (("xp", xp), ("xe", xe), ("wp", wp), ("we", we), ("sq", sq), ("w13", w13),
                    ("w2", np.asarray(L0_ffn_w2)), ("vecs", vecs), ("rows", rows), ("cst", cst)):
        a = np.ascontiguousarray(a)
        arrays[name] = a
        args.append(nc.dram_tensor(name, a.shape, mybir.dt.from_np(a.dtype), kind="ExternalInput").ap())
    res = nc.dram_tensor("out", (TOKENS, P), F32, kind="ExternalOutput").ap()
    tower(nc, *args, res)
    r = run_bass_kernel_spmd(nc, [arrays], core_ids=[0])
    return np.asarray(r.results[0]["out"]).reshape(IMAGES, T, P)
```
